# Optimizing a Trainium2 kernel written in Bass

```python
import numpy as np
import jax
import jax.numpy as jnp

def _softmax(x, axis=-1):
    return jax.nn.softmax(x, axis=axis)

def _gelu(x):
    return jax.nn.gelu(x, approximate=True)

def _silu(x):
    return jax.nn.silu(x)

def _sigmoid(x):
    return jax.nn.sigmoid(x)

def _layernorm(x, axis=-1, eps=1e-05):
    m = jnp.mean(x, axis=axis, keepdims=True)
    v = jnp.var(x, axis=axis, keepdims=True)
    return (x - m) / jnp.sqrt(v + eps)

def _scatter_add(tgt, idx, src, axis=0):
    return tgt.at[idx].add(src)

def _segment_sum(src, seg, n):
    return jax.ops.segment_sum(src, seg, n)
kernel_name = 'mk_seq_postln_d1_jaxref_r8_4c2d12'

def setup_inputs(seed: int=0):
    np.random.seed(seed)
    _w = jnp.asarray

    def _L0_attn_setup():
        import jax, jax.numpy as jnp
        import numpy as np
        HEADS = 4
        DIM_HEAD = 32
        EPS = 1e-05
        key = jax.random.key(seed)
        ks = jax.random.split(key, 6)
        b, n, dim = (8, 512, 128)
        hidden = HEADS * DIM_HEAD
        x = jax.random.normal(ks[0], (b, n, dim), dtype=jnp.float32)
        gamma = jnp.ones((1, 1, dim), dtype=jnp.float32)
        beta = jnp.zeros((1, 1, dim), dtype=jnp.float32)
        w_qkv = jax.random.normal(ks[1], (dim, hidden * 3), dtype=jnp.float32) / np.sqrt(dim)
        w_out = jax.random.normal(ks[2], (hidden, dim), dtype=jnp.float32) / np.sqrt(hidden)
        b_out = jnp.zeros((dim,), dtype=jnp.float32)
        return {'x': x, 'gamma': gamma, 'beta': beta, 'w_qkv': w_qkv, 'w_out': w_out, 'b_out': b_out}
    _L0_attn_in = _L0_attn_setup()

    def _L0_ffn_setup():
        import jax, jax.numpy as jnp
        import numpy as np
        B, S, D, H, E, K = (2, 256, 128, 256, 8, 2)
        key = jax.random.key(seed)
        ks = jax.random.split(key, 9)
        sc_d = 1.0 / np.sqrt(D)
        sc_h = 1.0 / np.sqrt(H)
        return {'x': jax.random.normal(ks[0], (B, S, D), dtype=jnp.float32), 'w_router': jax.random.normal(ks[1], (E, D), dtype=jnp.float32) * sc_d, 'Wg': jax.random.normal(ks[2], (E, H, D), dtype=jnp.float32) * sc_d, 'Wu': jax.random.normal(ks[3], (E, H, D), dtype=jnp.float32) * sc_d, 'Wd': jax.random.normal(ks[4], (E, D, H), dtype=jnp.float32) * sc_h, 'sg': jax.random.normal(ks[5], (H, D), dtype=jnp.float32) * sc_d, 'su': jax.random.normal(ks[6], (H, D), dtype=jnp.float32) * sc_d, 'sd': jax.random.normal(ks[7], (D, H), dtype=jnp.float32) * sc_h}
    _L0_ffn_in = _L0_ffn_setup()
    _d = {'L0_attn_x': _L0_attn_in['x'], 'L0_attn_gamma': _L0_attn_in['gamma'], 'L0_attn_beta': _L0_attn_in['beta'], 'L0_attn_w_qkv': _L0_attn_in['w_qkv'], 'L0_attn_w_out': _L0_attn_in['w_out'], 'L0_attn_b_out': _L0_attn_in['b_out'], 'L0_ffn_w_router': _L0_ffn_in['w_router'], 'L0_ffn_Wg': _L0_ffn_in['Wg'], 'L0_ffn_Wu': _L0_ffn_in['Wu'], 'L0_ffn_Wd': _L0_ffn_in['Wd'], 'L0_ffn_sg': _L0_ffn_in['sg'], 'L0_ffn_su': _L0_ffn_in['su'], 'L0_ffn_sd': _L0_ffn_in['sd']}
    _x0 = _d['L0_attn_x']
    _d['L0_attn_x'] = jax.random.normal(jax.random.fold_in(jax.random.key(seed), 1), (8, 512, 128), dtype=_x0.dtype)
    del _x0
    return _d

def reference(L0_attn_x, L0_attn_gamma, L0_attn_beta, L0_attn_w_qkv, L0_attn_w_out, L0_attn_b_out, L0_ffn_w_router, L0_ffn_Wg, L0_ffn_Wu, L0_ffn_Wd, L0_ffn_sg, L0_ffn_su, L0_ffn_sd):

    def _L0_attn_ref(x, gamma, beta, w_qkv, w_out, b_out):
        import jax, jax.numpy as jnp
        import numpy as np
        HEADS = 4
        DIM_HEAD = 32
        EPS = 1e-05
        b, n, dim = x.shape
        mean = jnp.mean(x, axis=2, keepdims=True)
        var = jnp.var(x, axis=2, keepdims=True)
        xn = (x - mean) / jnp.sqrt(var + EPS) * gamma + beta
        qkv = jnp.einsum('bnc,ck->bnk', xn, w_qkv)
        q, k, v = jnp.split(qkv, 3, axis=2)

        def to_heads(t):
            return t.reshape(b, n, HEADS, DIM_HEAD)
        q, k, v = (to_heads(q), to_heads(k), to_heads(v))
        q = q * DIM_HEAD ** (-0.5)
        k = jax.nn.softmax(k, axis=1)
        context = jnp.einsum('bnhd,bnhe->bhde', k, v)
        out = jnp.einsum('bhde,bnhd->bnhe', context, q)
        out = out.reshape(b, n, HEADS * DIM_HEAD)
        out = jnp.einsum('bnk,kc->bnc', out, w_out) + b_out
        return out + x

    def _L0_ffn_ref(x, w_router, Wg, Wu, Wd, sg, su, sd):
        import jax, jax.numpy as jnp
        import numpy as np
        B, S, D, H, E, K = (2, 256, 128, 256, 8, 2)
        b, s, d = x.shape
        xf = x.reshape(-1, d)
        logits = jnp.einsum('td,ed->te', xf, w_router)
        probs = jax.nn.softmax(logits, axis=-1)
        topw, topi = jax.lax.top_k(probs, K)
        topw = topw / jnp.sum(topw, axis=-1, keepdims=True)
        comb = jnp.sum(topw[..., None] * jax.nn.one_hot(topi, E, dtype=xf.dtype), axis=1)
        shared = jnp.einsum('th,dh->td', jax.nn.silu(jnp.einsum('td,hd->th', xf, sg)) * jnp.einsum('td,hd->th', xf, su), sd)
        h1 = jax.nn.silu(jnp.einsum('td,ehd->teh', xf, Wg))
        h2 = jnp.einsum('td,ehd->teh', xf, Wu)
        eo = jnp.einsum('teh,edh->ted', h1 * h2, Wd)
        routed = jnp.einsum('te,ted->td', comb, eo)
        return (routed + shared).reshape(b, s, d)
    x = L0_attn_x
    x = _layernorm(x + _L0_attn_ref(x, L0_attn_gamma, L0_attn_beta, L0_attn_w_qkv, L0_attn_w_out, L0_attn_b_out), axis=-1)
    x = _layernorm(x + _L0_ffn_ref(x, L0_ffn_w_router, L0_ffn_Wg, L0_ffn_Wu, L0_ffn_Wd, L0_ffn_sg, L0_ffn_su, L0_ffn_sd), axis=-1)
    return x

_drawn_inputs = setup_inputs


def setup_inputs(seed=0):
    import zlib

    import numpy as np

    out = dict(_drawn_inputs(seed))
    spreads = {'L0_attn_gamma': (1.0, 0.2), 'L0_attn_beta': (0.0, 0.1), 'L0_attn_b_out': (0.0, 0.1)}
    factors = {}
    for name, (base, spread) in spreads.items():
        noise = np.random.default_rng([zlib.crc32(name.encode()), seed]).standard_normal(out[name].shape)
        drawn = base * np.exp(spread * noise) if base else spread * noise
        out[name] = jnp.asarray(drawn.astype(out[name].dtype))
    for name, factor in factors.items():
        out[name] = (out[name] * factor).astype(out[name].dtype)
    return out
```

```python
import concourse.bass as bass
from concourse import mybir
from contextlib import ExitStack



class Tile:

    def __init__(self, t, parity):
        self.t, self.p = t, parity

    def next(self):
        return Tile(self.t + 1, 1 - self.p)

    def prev(self):
        return Tile(self.t - 1, 1 - self.p)


def build(nc, x_d, small_d, bout_d, experts_d, out_d):
    F32, F32R, U32 = mybir.dt.float32, mybir.dt.float32r, mybir.dt.uint32
    ALU = mybir.AluOpType
    ACT = mybir.ActivationFunctionType
    AX = mybir.AxisListType

    B, N, D = x_d.shape
    P = 128
    C = N // P
    NX = experts_d.shape[0]
    E = NX - 1
    H = (experts_d.shape[2]) // 3
    HH = H // P
    NH = NX * HH
    NG = E * HH
    HEADS, DH = 4, 32
    EPS = 1e-5
    LAST = B - 1
    R = 3
    LAG = 3
    WD = 2 * H

    ctx = ExitStack()
    with ctx:
        def sb(name, shape, dt=F32):
            return ctx.enter_context(nc.sbuf_tensor(name, shape, dt))

        def sem(name):
            return ctx.enter_context(nc.semaphore(name))

        w_raw = sb("w_raw", [P, NX, 3 * H])
        w_hi = sb("w_hi", [P, NX, 3 * H], F32R)
        w_lo = sb("w_lo", [P, NX, 3 * H], F32R)
        small = sb("small", [P, 4 * P + E + 2])
        wk, wv, wout, wqT = (small[:, i * P:(i + 1) * P] for i in range(4))
        router_raw = small[:, 4 * P:4 * P + E]
        gamma = small[:, 4 * P + E:4 * P + E + 1]
        beta = small[:, 4 * P + E + 1:4 * P + E + 2]
        router = sb("router", [P, 2 * E], F32R)
        bout = sb("bout", [P, D])
        ident = sb("ident", [P, P])
        head_mask = sb("head_mask", [P, P])
        iota = sb("iota", [P, E], U32)
        neg_half = sb("neg_half", [P, C])
        euler = sb("euler", [P, C])

        x_all = sb("x_all", [P, B, C, D])
        stats_all = sb("stats_all", [P, B, C, 6])
        mv_all = sb("mv_all", [P, B, C, 2])
        vareps_all = sb("vareps_all", [P, B, C])
        rstd_all = sb("rstd_all", [P, B, C])
        xhat = sb("xhat", [P, C, D])
        xnT = sb("xnT", [P, N])
        expT = sb("expT", [P, N])
        kneg = sb("kneg", [P, 1])
        ksum = sb("ksum", [P, 1])
        kinv = sb("kinv", [P, 1])
        probT = sb("probT", [P, N])
        prob = sb("prob", [P, C, P])
        av = sb("av", [P, P])
        ctxm = sb("ctxm", [P, P])
        ctxo = sb("ctxo", [P, D])
        mix = sb("mix", [P, D])
        x_plus = sb("x_plus", [P, C, D])
        x_twice = sb("x_twice", [P, C, D])
        res = sb("res", [P, C, D])
        stats = sb("stats", [P, C, 6])
        mv = sb("mv", [P, C, 2])
        vareps = sb("vareps", [P, C])
        rstd = sb("rstd", [P, C])
        x1 = [sb(f"x1_{i}", [P, C, D]) for i in range(2)]
        x1_hi = [sb(f"x1_hi{i}", [P, N], F32R) for i in range(2)]
        x1_lo = [sb(f"x1_lo{i}", [P, N], F32R) for i in range(2)]

        logits = sb("logits", [P, C, E])
        logits_lo = sb("logits_lo", [P, C, E])
        top = sb("top", [P, C, 8])
        topi = sb("topi", [P, C, 8], U32)
        gap = sb("gap", [P, C])
        gap_exp = sb("gap_exp", [P, C])
        den = sb("den", [P, C])
        weights = sb("weights", [P, C, 2])
        chosen = sb("chosen", [P, C, 2, E])
        chosen_w = sb("chosen_w", [P, C, 2, E])
        comb = sb("comb", [P, C, E])
        combT = sb("combT", [C * E, P])
        gate = sb("gate", [P, E, N])

        act_g = [sb(f"act_g{i}", [P, N]) for i in range(R)]
        hid = [sb(f"hid{i}", [P, N]) for i in range(R)]
        gated = [sb(f"gated{i}", [P, N]) for i in range(R)]
        h_hi = [sb(f"h_hi{i}", [P, N], F32R) for i in range(R)]
        h_lo = [sb(f"h_lo{i}", [P, N], F32R) for i in range(R)]

        yT = sb("yT", [P, N])
        res2 = sb("res2", [P, C, D])
        stats2 = sb("stats2", [P, C, 6])
        mv2 = sb("mv2", [P, C, 2])
        vareps2 = sb("vareps2", [P, C])
        rstd2 = sb("rstd2", [P, C])
        out_sb = sb("out_sb", [P, C, D])

        def bank(name):
            return ctx.enter_context(nc.psum_tensor(name, [P, N], F32))

        ps_g = [bank(f"ps_g{i}") for i in range(R)]
        ps_u = [bank(f"ps_u{i}") for i in range(R)]
        ps_y = bank("ps_y")
        ps_a = bank("ps_a")

        comb_dram = nc.dram_tensor("comb_dram", [B, C, E, P], F32, kind="Internal").ap()

        x_loaded = [sem(f"x_loaded{b}") for b in range(B)]
        small_loaded, bout_loaded = sem("small_loaded"), sem("bout_loaded")
        w_loaded = [sem(f"w_loaded{i}") for i in range(NX)]
        w_hi_done, w_lo_dve, w_lo_pool = sem("w_hi_done"), sem("w_lo_dve"), sem("w_lo_pool")
        router_hi_done, router_lo_done = sem("router_hi_done"), sem("router_lo_done")
        ident_zero, consts_done, mask_done = sem("ident_zero"), sem("consts_done"), sem("mask_done")
        mask_zero = sem("mask_zero")
        stats_all_done, mv_all_done = sem("stats_all_done"), sem("mv_all_done")
        vareps_all_done, rstd_all_done = sem("vareps_all_done"), sem("rstd_all_done")
        xhat_done, xhatT_done, xn_done = sem("xhat_done"), sem("xhatT_done"), sem("xn_done")
        k_done, kmax_done, exp_done = sem("k_done"), sem("kmax_done"), sem("exp_done")
        kinv_done, probT_done, probt_done = sem("kinv_done"), sem("probT_done"), sem("probt_done")
        prob_done, av_done, av_copied = sem("prob_done"), sem("av_done"), sem("av_copied")
        ctx_done, ctxm_done = sem("ctx_done"), sem("ctxm_done")
        ctxo_done, ctxo_copied = sem("ctxo_done"), sem("ctxo_copied")
        mix_done, mix_copied, attn_done = sem("mix_done"), sem("mix_copied"), sem("attn_done")
        x_plus_done, x_twice_done, res_done = sem("x_plus_done"), sem("x_twice_done"), sem("res_done")
        stats_done, mv_done = sem("stats_done"), sem("mv_done")
        vareps_done, rstd_done, x1_done = sem("vareps_done"), sem("rstd_done"), sem("x1_done")
        x1T_done, x1_hi_done, x1_lo_done = sem("x1T_done"), sem("x1_hi_done"), sem("x1_lo_done")
        logits_done, logits_copied = sem("logits_done"), sem("logits_copied")
        logits_lo_copied = sem("logits_lo_copied")
        top_done, gap_done, gap_exp_done = sem("top_done"), sem("gap_done"), sem("gap_exp_done")
        den_done, w0_done, weights_done = sem("den_done"), sem("w0_done"), sem("weights_done")
        topi_done, chosen_done, chosen_w_done = sem("topi_done"), sem("chosen_done"), sem("chosen_w_done")
        comb_done, combT_done, combT_copied = sem("comb_done"), sem("combT_done"), sem("combT_copied")
        comb_stored = sem("comb_stored")
        gate_loaded = [sem(f"gate_loaded{e}") for e in range(E)]
        g_done, u_done, silu_done = sem("g_done"), sem("u_done"), sem("silu_done")
        hid_done, gated_done = sem("hid_done"), sem("gated_done")
        h_hi_done, h_lo_done, down_done = sem("h_hi_done"), sem("h_lo_done"), sem("down_done")
        y_copied, y_turned, res2_done = sem("y_copied"), sem("y_turned"), sem("res2_done")
        stats2_done, mv2_done = sem("stats2_done"), sem("mv2_done")
        vareps2_done, rstd2_done = sem("vareps2_done"), sem("rstd2_done")
        out_ready, out_stored = sem("out_ready"), sem("out_stored")

        class Slots:
            XT, K, Y, PROB, AV, CTX, CTXO, MIX, ATT, X1T, ROUTE, COMB = 0, 1, 4, 5, 6, 7, 8, 9, 10, 14, 15, 17

        class FirstSlots(Slots):
            ROUTE0, XT, COMB0, K = 0, 1, 2, 3
            PROB, AV, CTX, CTXO, MIX, ATT, X1T, ROUTE, COMB = 6, 7, 8, 9, 10, 11, 14, 15, 17

        SPLITS_DVE, SPLITS_POOL = [0, 1, 6, 7, 8], [2, 3, 4, 5]

        def bcast(ap, shape):
            return ap.to_broadcast(shape)

        waited = {e: sem(f"waited_{n}") for e, n in ((nc.vector, "dve"), (nc.gpsimd, "pool"), (nc.sync, "sp"))}

        def wait_apart(eng, semaphore, value):
            eng.wait_ge(semaphore, value)
            if not isinstance(value, int):
                eng.sem_inc(waited[eng], 1)

        block = ctx.enter_context(nc.Block())

        def steps(eng, step):
            step(Tile(0, 0), True, False)
            with eng.Fori(0, (B - 2) // 2) as i:
                step(Tile(i * 2 + 1, 1), False, False)
                step(Tile(i * 2 + 2, 0), False, False)
            step(Tile(LAST, LAST % 2), False, True)

        @block.sync
        def _(sp):
            x_view = x_d.rearrange("b (c p) d -> b p c d", p=P)

            def load_x(b):
                sp.dma_start(x_all[:, b, :, :], x_view[b]).then_inc(x_loaded[b], 16)

            def load_expert(e):
                sp.dma_start(w_raw[:, e, :], experts_d[e]).then_inc(w_loaded[e], 16)

            load_x(0)
            sp.dma_start(small[:, :], small_d).then_inc(small_loaded, 16)
            load_expert(0)
            sp.dma_start(bout[:, :], bout_d.partition_broadcast(P)).then_inc(bout_loaded, 16)
            load_x(1)
            for e in range(1, NX):
                load_expert(e)
            for b in range(2, B):
                load_x(b)

            def spread_gates(a):
                wait_apart(sp, combT_copied, a.t + 1)
                sp.dma_start(comb_dram[a.t].rearrange("c e n -> (c e) n"), combT[:, :]).then_inc(comb_stored, 16)
                wait_apart(sp, comb_stored, a.t * 16 + 16)
                for e in range(E):
                    if not (isinstance(a.t, int) and a.t == 0):
                        sp.wait_ge(gated_done, (a.t - 1) * NG + HH * (e + 1))
                    sp.dma_start(gate[:, e, :].rearrange("p (c n) -> p c n", c=C),
                                 comb_dram[a.t, :, e, :].partition_broadcast(P))\
                      .then_inc(gate_loaded[e], 16)

            def store(t):
                wait_apart(sp, out_ready, t.t + 1)
                sp.dma_start(out_d.rearrange("b (c p) d -> b p c d", p=P)[t.t], out_sb[:, :, :])\
                  .then_inc(out_stored, 16)

            def step(t, first, last):
                if first:
                    spread_gates(t)
                else:
                    store(t.prev())
                if not last:
                    spread_gates(t.next())

            steps(sp, step)
            store(Tile(LAST, 0))
            sp.wait_ge(out_stored, 16 * B)

        @block.gpsimd
        def _(pool):
            pool.memset(ident[:, :], 0.0).then_inc(ident_zero, 1)
            pool.memset(neg_half[:, :], -0.5)
            pool.memset(euler[:, :], 2.718281828459045)
            pool.iota(iota[:, :], pattern=[[1, E]], base=0, channel_multiplier=0)
            pool.wait_ge(ident_zero, 1)
            pool.affine_select(out=ident[:, :], in_=ident[:, :], compare_op=ALU.not_equal, fill=1.0,
                               base=0, pattern=[[-1, P]], channel_multiplier=1).then_inc(consts_done, 1)
            pool.wait_ge(consts_done, 1)

            def inverse_root(out, var, tmp, var_ready, n, tmp_done, done):
                wait_apart(pool, var_ready, n)
                pool.tensor_scalar(tmp, var, EPS, None, ALU.add).then_inc(tmp_done, 1)
                pool.wait_ge(tmp_done, n)
                pool.tensor_tensor(out, tmp, neg_half[:, :], ALU.pow).then_inc(done, 1)

            def twice_x(a):
                if isinstance(a.t, int) and a.t < 2:
                    pool.wait_ge(x_loaded[a.t], 16)
                    pool.wait_ge(bout_loaded, 16)
                if not (isinstance(a.t, int) and a.t == 0):
                    wait_apart(pool, res_done, a.t)
                pool.tensor_tensor(x_plus[:, :, :], x_all[:, a.t, :, :],
                                   bout[:, None, :].to_broadcast([P, C, D]), ALU.add).then_inc(x_plus_done, 1)
                wait_apart(pool, x_plus_done, a.t + 1)
                pool.tensor_tensor(x_twice[:, :, :], x_plus[:, :, :], x_all[:, a.t, :, :], ALU.add)\
                    .then_inc(x_twice_done, 1)

            def norm_x(b):
                inverse_root(rstd_all[:, b, :], mv_all[:, b, :, 1], vareps_all[:, b, :],
                             mv_all_done, b + 1, vareps_all_done, rstd_all_done)

            def split_weights(e):
                pool.wait_ge(w_hi_done, e + 1)
                pool.tensor_tensor(w_lo[:, e, :], w_raw[:, e, :], w_hi[:, e, :].bitcast(F32), ALU.subtract)\
                    .then_inc(w_lo_pool, 1)

            def norm1(a):
                inverse_root(rstd[:, :], mv[:, :, 1], vareps[:, :], mv_done, a.t + 1, vareps_done, rstd_done)

            def gap_power(a):
                pool.wait_ge(gap_done, a.t + 1)
                pool.tensor_tensor(gap_exp[:, :], euler[:, :], gap[:, :], ALU.pow).then_inc(gap_exp_done, 1)

            def norm2(t):
                inverse_root(rstd2[:, :], mv2[:, :, 1], vareps2[:, :], mv2_done, t.t + 1, vareps2_done, rstd2_done)

            norm_x(0)
            twice_x(Tile(0, 0))
            norm_x(1)
            for e in SPLITS_POOL:
                split_weights(e)
            norm1(Tile(0, 0))

            def gate_half(t, j):
                e = j // HH - 1
                n = t.t * NH + j
                if j % HH == 0:
                    pool.wait_ge(gate_loaded[e], t.t * 16 + 16)
                pool.wait_ge(hid_done, n + 1)
                if not (isinstance(n, int) and n < R):
                    pool.wait_ge(h_lo_done, n - R + 1)
                pool.tensor_tensor(gated[j % R][:, :], hid[j % R][:, :], gate[:, e, :], ALU.mult)\
                    .then_inc(gated_done, 1)

            def step(t, first, last):
                a = None if last else t.next()
                S = FirstSlots if first else Slots
                for j in range(NH):
                    if j >= HH:
                        gate_half(t, j)
                    if first:
                        if j == S.ROUTE0:
                            gap_power(t)
                        if j >= 3 and j % 2 and j // 2 + 1 < B:
                            norm_x(j // 2 + 1)
                    if not last:
                        if j == 1:
                            twice_x(a)
                        if j == S.ATT + 1:
                            norm1(a)
                        if j == S.ROUTE:
                            gap_power(a)
                    if not first and j == S.Y + 4:
                        norm2(t.prev())

            steps(pool, step)
            norm2(Tile(LAST, 0))

        @block.scalar
        def _(act):
            act.wait_ge(small_loaded, 16)
            act.activation(router[:, 0:E], router_raw, ACT.Copy).then_inc(router_hi_done, 1)

            def split_weights(e):
                act.wait_ge(w_loaded[e], 16)
                act.activation(w_hi[:, e, :], w_raw[:, e, :], ACT.Copy).then_inc(w_hi_done, 1)

            def norm_out(a):
                act.wait_ge(xhatT_done, a.t + 1)
                act.activation(xnT[:, :], ps_a[:, :], ACT.Identity, bias=beta, scale=gamma)\
                   .then_inc(xn_done, 1)

            def exps(a):
                act.wait_ge(kmax_done, a.t + 1)
                act.activation(expT[:, :], ps_a[:, :], ACT.Exp, bias=kneg[:, :], accum_out=ksum[:, :])\
                   .then_inc(exp_done, 1)

            def copy(a, dst, src, ready, done):
                act.wait_ge(ready, a.t + 1)
                act.activation(dst, src, ACT.Copy).then_inc(done, 1)

            def copy_prob(a):
                copy(a, prob[:, :, :].rearrange("p c d -> p (c d)"), ps_a[:, :], probt_done, prob_done)

            def copy_ctxo(a):
                copy(a, ctxo[:, :], ps_a[:, 0:D], ctxo_done, ctxo_copied)

            def copy_mix(a):
                copy(a, mix[:, :], ps_a[:, 0:D], mix_done, mix_copied)

            def x1_high(a):
                copy(a, x1_hi[a.p][:, :], ps_a[:, :], x1T_done, x1_hi_done)

            def copy_combT(a):
                if not (isinstance(a.t, int) and a.t == 0):
                    act.wait_ge(comb_stored, a.t * 16)
                copy(a, combT[:, :], ps_a[0:C * E, 0:P], combT_done, combT_copied)

            def copy_y(t):
                act.wait_ge(down_done, t.t * NH + NH)
                act.activation(yT[:, :], ps_y[:, :], ACT.Copy).then_inc(y_copied, 1)

            zero = Tile(0, 0)
            norm_out(zero)
            split_weights(0)
            exps(zero)
            split_weights(1)
            split_weights(2)
            copy_prob(zero)
            split_weights(3)
            split_weights(4)
            split_weights(5)
            copy_ctxo(zero)
            copy_mix(zero)
            for e in range(6, NX):
                split_weights(e)
            x1_high(zero)

            def silu(t, j):
                n = t.t * NH + j
                act.wait_ge(g_done, n + 1)
                if not (isinstance(n, int) and n < R):
                    act.wait_ge(hid_done, n - R + 1)
                act.activation(act_g[j % R][:, :], ps_g[j % R][:, :], ACT.Silu).then_inc(silu_done, 1)

            def high(t, j):
                n = t.t * NH + j
                if j < HH:
                    act.wait_ge(hid_done, n + 1)
                else:
                    act.wait_ge(gated_done, t.t * NG + j - HH + 1)
                if not (isinstance(n, int) and n < R):
                    act.wait_ge(down_done, n - R + 1)
                act.activation(h_hi[j % R][:, :], gated[j % R][:, :], ACT.Copy).then_inc(h_hi_done, 1)

            def step(t, first, last):
                a = None if last else t.next()
                S = FirstSlots if first else Slots
                for j in range(NH):
                    if not first and j == LAG:
                        copy_y(t.prev())
                    if first and j == S.COMB0 + 1:
                        copy_combT(t)
                    if not last:
                        if j == S.XT + 1:
                            norm_out(a)
                        if j == S.PROB + 1:
                            copy_prob(a)
                        if j == S.CTXO + 1:
                            copy_ctxo(a)
                        if j == S.MIX + 1:
                            copy_mix(a)
                        if j == S.X1T + 1:
                            x1_high(a)
                    silu(t, j)
                    if j > 0:
                        high(t, j - 1)
                    elif not first:
                        high(t.prev(), NH - 1)
                    if not last and j == S.K + 1:
                        exps(a)
                if not last:
                    copy_combT(a)

            steps(act, step)
            high(Tile(LAST, 1), NH - 1)
            copy_y(Tile(LAST, 1))

        @block.vector
        def _(dve):
            dve.memset(head_mask[:, :], 0.0).then_inc(mask_zero, 1)
            dve.wait_ge(mask_zero, 1)
            for h in range(HEADS):
                s = slice(h * DH, (h + 1) * DH)
                last = dve.memset(head_mask[s, s], DH ** -0.5)
            last.then_inc(mask_done, 1)

            def norm_stats(x, st, m, ready, value, n, st_done, m_done):
                dve.wait_ge(ready, value)
                for c in range(C):
                    last = dve.bn_stats(st[:, c, :], x[:, c, :])
                last.then_inc(st_done, 1)
                wait_apart(dve, st_done, n)
                for c in range(C):
                    last = dve.bn_aggr(m[:, c, :], st[:, c, :])
                last.then_inc(m_done, 1)

            def normalise(a):
                dve.wait_ge(rstd_all_done, a.t + 1 if isinstance(a.t, int) and a.t < 2 else B)
                for c in range(C):
                    last = dve.tensor_scalar(xhat[:, c, :], x_all[:, a.t, c, :], mv_all[:, a.t, c, 0:1],
                                             rstd_all[:, a.t, c:c + 1], ALU.subtract, ALU.mult)
                last.then_inc(xhat_done, 1)

            def key_max(a):
                dve.wait_ge(k_done, a.t + 1)
                dve.tensor_reduce(kneg[:, :], ps_a[:, :], AX.X, ALU.max, negate=True).then_inc(kmax_done, 1)

            def probabilities(a):
                dve.wait_ge(exp_done, a.t + 1)
                dve.reciprocal(kinv[:, :], ksum[:, :]).then_inc(kinv_done, 1)
                dve.wait_ge(kinv_done, a.t + 1)
                dve.tensor_scalar(probT[:, :], expT[:, :], kinv[:, :], None, ALU.mult).then_inc(probT_done, 1)

            def copy_av(a):
                dve.wait_ge(av_done, a.t + 1)
                dve.tensor_scalar(av[:, :], ps_a[:, 0:P], gamma, beta, ALU.mult, ALU.add)\
                   .then_inc(av_copied, 1)

            def mask_heads(a):
                dve.wait_ge(ctx_done, a.t + 1)
                dve.tensor_tensor(ctxm[:, :], ps_a[:, 0:P], head_mask[:, :], ALU.mult).then_inc(ctxm_done, 1)

            def residual(a):
                dve.wait_ge(attn_done, a.t + 1)
                dve.wait_ge(x_twice_done, a.t + 1)
                dve.tensor_tensor(res[:, :, :].rearrange("p c d -> p (c d)"), ps_a[:, :],
                                  x_twice[:, :, :].rearrange("p c d -> p (c d)"), ALU.add).then_inc(res_done, 1)
                norm_stats(res, stats, mv, res_done, a.t + 1, a.t + 1, stats_done, mv_done)

            def first_norm(a):
                dve.wait_ge(rstd_done, a.t + 1)
                for c in range(C):
                    last = dve.tensor_scalar(x1[a.p][:, c, :], res[:, c, :], mv[:, c, 0:1], rstd[:, c:c + 1],
                                             ALU.subtract, ALU.mult)
                last.then_inc(x1_done, 1)

            def x1_low(a):
                dve.wait_ge(x1_hi_done, a.t + 1)
                dve.tensor_tensor(x1_lo[a.p][:, :], ps_a[:, :], x1_hi[a.p][:, :].bitcast(F32), ALU.subtract)\
                   .then_inc(x1_lo_done, 1)

            def best_two(a):
                dve.wait_ge(logits_done, a.t + 1)
                parts = ps_a[:, 0:C * 2 * E].rearrange("p (c two e) -> p c two e", c=C, two=2)
                dve.tensor_copy(logits_lo[:, :, :], parts[:, :, 1, :]).then_inc(logits_lo_copied, 1)
                dve.wait_ge(logits_lo_copied, a.t + 1)
                dve.tensor_tensor(logits[:, :, :], parts[:, :, 0, :], logits_lo[:, :, :], ALU.add)\
                   .then_inc(logits_copied, 1)
                wait_apart(dve, logits_copied, a.t + 1)
                for c in range(C):
                    last = dve.max(top[:, c, :], logits[:, c, :])
                last.then_inc(top_done, 1)
                dve.wait_ge(top_done, a.t + 1)
                dve.tensor_tensor(gap[:, :], top[:, :, 1], top[:, :, 0], ALU.subtract).then_inc(gap_done, 1)
                for c in range(C):
                    last = dve.max_index(topi[:, c, :], top[:, c, :], logits[:, c, :])
                last.then_inc(topi_done, 1)
                dve.wait_ge(topi_done, a.t + 1)
                dve.tensor_tensor(chosen[:, :, :, :], iota[:, None, None, :].to_broadcast([P, C, 2, E]),
                                  topi[:, :, 0:2, None].to_broadcast([P, C, 2, E]), ALU.is_equal)\
                   .then_inc(chosen_done, 1)

            def combine_weights(a):
                dve.wait_ge(gap_exp_done, a.t + 1)
                dve.tensor_scalar(den[:, :], gap_exp[:, :], 1.0, None, ALU.add).then_inc(den_done, 1)
                dve.wait_ge(den_done, a.t + 1)
                dve.reciprocal(weights[:, :, 0], den[:, :]).then_inc(w0_done, 1)
                dve.wait_ge(w0_done, a.t + 1)
                dve.tensor_tensor(weights[:, :, 1], gap_exp[:, :], weights[:, :, 0], ALU.mult)\
                   .then_inc(weights_done, 1)
                dve.wait_ge(weights_done, a.t + 1)
                dve.wait_ge(chosen_done, a.t + 1)
                dve.tensor_tensor(chosen_w[:, :, :, :], chosen[:, :, :, :],
                                  weights[:, :, :, None].to_broadcast([P, C, 2, E]), ALU.mult)\
                   .then_inc(chosen_w_done, 1)
                dve.wait_ge(chosen_w_done, a.t + 1)
                dve.tensor_tensor(comb[:, :, :], chosen_w[:, :, 0, :], chosen_w[:, :, 1, :], ALU.add)\
                   .then_inc(comb_done, 1)

            def last_residual(t):
                dve.wait_ge(y_turned, t.t + 1)
                dve.tensor_tensor(res2[:, :, :].rearrange("p c d -> p (c d)"), ps_a[:, :],
                                  x1[t.p][:, :, :].rearrange("p c d -> p (c d)"), ALU.add).then_inc(res2_done, 1)

            def last_stats(t):
                norm_stats(res2, stats2, mv2, res2_done, t.t + 1, t.t + 1, stats2_done, mv2_done)

            def last_norm(t):
                dve.wait_ge(rstd2_done, t.t + 1)
                if not (isinstance(t.t, int) and t.t == 0):
                    dve.wait_ge(out_stored, t.t * 16)
                for c in range(C):
                    last = dve.tensor_scalar(out_sb[:, c, :], res2[:, c, :], mv2[:, c, 0:1], rstd2[:, c:c + 1],
                                             ALU.subtract, ALU.mult)
                last.then_inc(out_ready, 1)

            def split_weights(e):
                dve.wait_ge(w_hi_done, e + 1)
                dve.tensor_tensor(w_lo[:, e, :], w_raw[:, e, :], w_hi[:, e, :].bitcast(F32), ALU.subtract)\
                   .then_inc(w_lo_dve, 1)

            def stats_x(b):
                norm_stats(x_all[:, b, :, :], stats_all[:, b, :, :], mv_all[:, b, :, :], x_loaded[b], 16,
                           b + 1, stats_all_done, mv_all_done)

            zero = Tile(0, 0)
            stats_x(0)
            dve.wait_ge(router_hi_done, 1)
            dve.tensor_tensor(router[:, E:], router_raw, router[:, 0:E].bitcast(F32), ALU.subtract)\
               .then_inc(router_lo_done, 1)
            normalise(zero)
            stats_x(1)
            split_weights(0)
            key_max(zero)
            split_weights(1)
            probabilities(zero)
            copy_av(zero)
            mask_heads(zero)
            residual(zero)
            first_norm(zero)
            x1_low(zero)

            def product(t, j):
                n = t.t * NH + j
                dve.wait_ge(silu_done, n + 1)
                dve.wait_ge(u_done, n + 1)
                if not (isinstance(n, int) and n < R):
                    dve.wait_ge(h_lo_done, n - R + 1)
                dst = gated if j < HH else hid
                dve.tensor_tensor(dst[j % R][:, :], ps_u[j % R][:, :], act_g[j % R][:, :], ALU.mult)\
                   .then_inc(hid_done, 1)

            def low(t, j):
                n = t.t * NH + j
                dve.wait_ge(h_hi_done, n + 1)
                dve.tensor_tensor(h_lo[j % R][:, :], gated[j % R][:, :], h_hi[j % R][:, :].bitcast(F32),
                                  ALU.subtract).then_inc(h_lo_done, 1)

            def step(t, first, last):
                a = None if last else t.next()
                S = FirstSlots if first else Slots
                for j in range(NH):
                    if first:
                        if j == S.ROUTE0 + 1:
                            best_two(t)
                        if j == S.COMB0:
                            combine_weights(t)
                    else:
                        if j == S.Y + 1:
                            last_residual(t.prev())
                        if j == S.Y + 4:
                            last_stats(t.prev())
                        if j == S.Y + 6:
                            last_norm(t.prev())
                    if not last:
                        if j == S.XT:
                            normalise(a)
                        if j == S.K + 1:
                            key_max(a)
                        if j == S.K + 3:
                            probabilities(a)
                        if j == S.AV + 1:
                            copy_av(a)
                        if j == S.CTX + 1:
                            mask_heads(a)
                        if j == S.ATT + 1:
                            residual(a)
                        if j == S.X1T:
                            first_norm(a)
                        if j == S.X1T + 1:
                            x1_low(a)
                        if j == S.ROUTE + 1:
                            best_two(a)
                        if j == S.COMB:
                            combine_weights(a)
                    if j >= 2:
                        low(t, j - 2)
                    elif not first:
                        low(t.prev(), NH - 2 + j)
                    product(t, j)
                    if first and j in (2, 3, 4):
                        split_weights(SPLITS_DVE[j])
                    if first and j >= 2 and j % 2 == 0 and j // 2 + 1 < B:
                        stats_x(j // 2 + 1)

            steps(dve, step)
            low(Tile(LAST, 1), NH - 2)
            low(Tile(LAST, 1), NH - 1)
            last_residual(Tile(LAST, 1))
            last_stats(Tile(LAST, 1))
            last_norm(Tile(LAST, 1))

        @block.tensor
        def _(pe):
            def turn(dst, src):
                for c in range(C):
                    last = pe.transpose(dst[:, c * P:(c + 1) * P], src(c), ident[:, :])
                return last

            def turn_x(a):
                pe.wait_ge(xhat_done, a.t + 1)
                if isinstance(a.t, int) and a.t == 1:
                    pe.wait_ge(logits_copied, 1)
                elif not (isinstance(a.t, int) and a.t == 0):
                    pe.wait_ge(combT_copied, a.t)
                turn(ps_a, lambda c: xhat[:, c, :]).then_inc(xhatT_done, 1)

            def keys(a):
                pe.wait_ge(xn_done, a.t + 1)
                if isinstance(a.t, int) and a.t == 1:
                    pe.wait_ge(combT_copied, 1)
                pe.matmul(ps_a[:, :], wk, xnT[:, :], start=True, stop=True).then_inc(k_done, 1)

            def turn_prob(a):
                pe.wait_ge(probT_done, a.t + 1)
                if not (isinstance(a.t, int) and a.t < 2):
                    pe.wait_ge(res2_done, a.t - 1)
                turn(ps_a, lambda c: probT[:, c * P:(c + 1) * P]).then_inc(probt_done, 1)

            def weigh_x(a):
                pe.wait_ge(prob_done, a.t + 1)
                for c in range(C):
                    last = pe.matmul(ps_a[:, 0:P], xhat[:, c, :], prob[:, c, :], start=c == 0, stop=c == C - 1)
                last.then_inc(av_done, 1)

            def context(a):
                pe.wait_ge(av_copied, a.t + 1)
                pe.matmul(ps_a[:, 0:P], wv, av[:, :], start=True, stop=True).then_inc(ctx_done, 1)

            def context_out(a):
                pe.wait_ge(ctxm_done, a.t + 1)
                pe.matmul(ps_a[:, 0:D], ctxm[:, :], wout, start=True, stop=True).then_inc(ctxo_done, 1)

            def mix_queries(a):
                pe.wait_ge(ctxo_copied, a.t + 1)
                pe.matmul(ps_a[:, 0:D], wqT, ctxo[:, :], start=True, stop=True).then_inc(mix_done, 1)

            def attend(a):
                pe.wait_ge(mix_copied, a.t + 1)
                for c in range(C):
                    last = pe.matmul(ps_a[:, c * D:(c + 1) * D], xnT[:, c * P:(c + 1) * P], mix[:, :],
                                     start=True, stop=True)
                last.then_inc(attn_done, 1)

            def turn_x1(a):
                pe.wait_ge(x1_done, a.t + 1)
                turn(ps_a, lambda c: x1[a.p][:, c, :]).then_inc(x1T_done, 1)

            def route(a):
                pe.wait_ge(x1_lo_done, a.t + 1)
                for c in range(C):
                    n, at = slice(c * P, (c + 1) * P), c * 2 * E
                    pe.matmul(ps_a[:, at:at + 2 * E], x1_hi[a.p][:, n], router[:, :],
                              start=True, stop=False, skip_group_check=True)
                    last = pe.matmul(ps_a[:, at:at + E], x1_lo[a.p][:, n], router[:, 0:E],
                                     start=False, stop=True, skip_group_check=True)
                last.then_inc(logits_done, 1)

            def turn_comb(a):
                pe.wait_ge(comb_done, a.t + 1)
                if isinstance(a.t, int) and a.t == 0:
                    pe.wait_ge(xn_done, 2)
                pe.transpose(ps_a[0:C * E, 0:P], comb[:, :, :].rearrange("p c e -> p (c e)"), ident[:, :])\
                    .then_inc(combT_done, 1)

            def turn_y(t, ready=None):
                pe.wait_ge(y_copied, t.t + 1)
                if ready:
                    pe.wait_ge(*ready)
                turn(ps_a, lambda c: yT[:, c * P:(c + 1) * P]).then_inc(y_turned, 1)

            def three(dst, e, col, hi, lo, start, stop):
                w = slice(col, col + P)
                pe.matmul(dst, w_hi[:, e, w], hi, start=start, stop=False)
                pe.matmul(dst, w_hi[:, e, w], lo, start=False, stop=False)
                return pe.matmul(dst, w_lo[:, e, w], hi, start=False, stop=stop)

            def up(t, j, first):
                e, h = j // HH, j % HH
                n = t.t * NH + j
                if j == 0:
                    pe.wait_ge(x1_lo_done, t.t + 1)
                if first and h == 0:
                    if e in SPLITS_DVE:
                        pe.wait_ge(w_lo_dve, SPLITS_DVE.index(e) + 1)
                    else:
                        pe.wait_ge(w_lo_pool, SPLITS_POOL.index(e) + 1)
                free = not (isinstance(n, int) and n < R)
                if free:
                    pe.wait_ge(silu_done, n - R + 1)
                three(ps_g[j % R][:, :], e, h * P, x1_hi[t.p][:, :], x1_lo[t.p][:, :], True, True)\
                    .then_inc(g_done, 1)
                if free:
                    pe.wait_ge(hid_done, n - R + 1)
                three(ps_u[j % R][:, :], e, H + h * P, x1_hi[t.p][:, :], x1_lo[t.p][:, :], True, True)\
                    .then_inc(u_done, 1)

            def down(t, j):
                e, h = j // HH, j % HH
                pe.wait_ge(h_lo_done, t.t * NH + j + 1)
                if j == 0 and not (isinstance(t.t, int) and t.t == 0):
                    pe.wait_ge(y_copied, t.t)
                three(ps_y[:, :], e, WD + h * P, h_hi[j % R][:, :], h_lo[j % R][:, :], j == 0, j == NH - 1)\
                    .then_inc(down_done, 1)

            zero = Tile(0, 0)
            pe.wait_ge(consts_done, 1)
            turn_x(zero)
            pe.wait_ge(small_loaded, 16)
            keys(zero)
            turn_prob(zero)
            weigh_x(zero)
            context(zero)
            context_out(zero)
            mix_queries(zero)
            attend(zero)
            turn_x1(zero)
            pe.wait_ge(router_lo_done, 1)

            def step(t, first, last):
                a = None if last else t.next()
                S = FirstSlots if first else Slots
                for j in range(NH):
                    up(t, j, first)
                    if j == LAG + 1:
                        down(t, 0)
                    if j > LAG:
                        down(t, j - LAG)
                    elif j < LAG and not first:
                        down(t.prev(), NH - LAG + j)
                    if first:
                        if j == S.ROUTE0:
                            route(t)
                        if j == S.COMB0:
                            turn_comb(t)
                    if not first and j == S.Y:
                        turn_y(t.prev(), None if last else (exp_done, a.t + 1))
                    if not last:
                        if j == S.XT:
                            turn_x(a)
                        if j == S.K:
                            keys(a)
                        if j == S.PROB:
                            turn_prob(a)
                        if j == S.AV:
                            weigh_x(a)
                        if j == S.CTX:
                            context(a)
                        if j == S.CTXO:
                            context_out(a)
                        if j == S.MIX:
                            mix_queries(a)
                        if j == S.ATT:
                            attend(a)
                        if j == S.X1T:
                            turn_x1(a)
                        if j == S.ROUTE:
                            route(a)
                        if j == S.COMB:
                            turn_comb(a)

            steps(pe, step)
            end = Tile(LAST, 1)
            for j in range(NH - LAG, NH):
                down(end, j)
            turn_y(end)


def kernel(**inputs):
    import numpy as np
    import concourse.bacc as bacc
    from concourse import mybir as mb
    from concourse.bass_utils import run_bass_kernel_spmd

    a = {k: np.asarray(v) for k, v in inputs.items()}
    D = a["L0_attn_x"].shape[2]
    hidden = a["L0_attn_w_qkv"].shape[1] // 3
    w = a["L0_attn_w_qkv"]

    def up(m):
        return np.swapaxes(m, -1, -2)

    def down(m):
        m = np.swapaxes(m, -1, -2)
        m = m.reshape(*m.shape[:-2], m.shape[-2] // 128, 128, D)
        m = np.swapaxes(m, -3, -2)
        return m.reshape(*m.shape[:-2], -1)

    shared = np.concatenate([up(a["L0_ffn_sg"]), up(a["L0_ffn_su"]), down(a["L0_ffn_sd"])], axis=-1)
    routed = np.concatenate([up(a["L0_ffn_Wg"]), up(a["L0_ffn_Wu"]), down(a["L0_ffn_Wd"])], axis=-1)
    small = [w[:, hidden:2 * hidden], w[:, 2 * hidden:], a["L0_attn_w_out"], w[:, 0:hidden].T,
             a["L0_ffn_w_router"].T, a["L0_attn_gamma"].reshape(D, 1), a["L0_attn_beta"].reshape(D, 1)]
    arrays = {
        "x": a["L0_attn_x"],
        "small": np.concatenate(small, axis=1),
        "bout": a["L0_attn_b_out"],
        "experts": np.concatenate([shared[None], routed], axis=0),
    }
    arrays = {k + "_in": np.ascontiguousarray(v) for k, v in arrays.items()}
    nc = bacc.Bacc("TRN2", target_bir_lowering=False, num_devices=1)
    args = [nc.dram_tensor(k, v.shape, mb.dt.from_np(v.dtype), kind="ExternalInput").ap()
            for k, v in arrays.items()]
    out = nc.dram_tensor("out", a["L0_attn_x"].shape, mb.dt.float32, kind="ExternalOutput").ap()
    build(nc, *args, out)
    r = run_bass_kernel_spmd(nc, [arrays], core_ids=[0])
    return r.results[0]["out"]
```

```python
import concourse.bass as bass
from concourse import mybir
from contextlib import ExitStack



class Tile:

    def __init__(self, t, parity):
        self.t, self.p = t, parity

    def next(self):
        return Tile(self.t + 1, 1 - self.p)

    def prev(self):
        return Tile(self.t - 1, 1 - self.p)


def build(nc, x_d, small_d, bout_d, experts_d, out_d):
    F32, F32R, U32 = mybir.dt.float32, mybir.dt.float32r, mybir.dt.uint32
    ALU = mybir.AluOpType
    ACT = mybir.ActivationFunctionType
    AX = mybir.AxisListType

    B, N, D = x_d.shape
    P = 128
    C = N // P
    NX = experts_d.shape[0]
    E = NX - 1
    H = (experts_d.shape[2]) // 3
    HH = H // P
    NH = NX * HH
    NG = E * HH
    HEADS, DH = 4, 32
    EPS = 1e-5
    LAST = B - 1
    R = 3
    RH = 6
    LAG = 4
    WD = 2 * H

    ctx = ExitStack()
    with ctx:
        def sb(name, shape, dt=F32):
            return ctx.enter_context(nc.sbuf_tensor(name, shape, dt))

        def sem(name):
            return ctx.enter_context(nc.semaphore(name))

        w_hi = sb("w_hi", [P, NX, 3 * H], F32R)
        w_lo = sb("w_lo", [P, NX, 3 * H], F32R)
        w_loaded_flat = sb("w_raw", [P, NX * 3 * H])
        w_raw = w_loaded_flat[:, :].rearrange("p (e w) -> p e w", e=NX)
        small = sb("small", [P, 4 * P + E + 2])
        wk, wv, wout, wqT = (small[:, i * P:(i + 1) * P] for i in range(4))
        router_raw = small[:, 4 * P:4 * P + E]
        gamma = small[:, 4 * P + E:4 * P + E + 1]
        beta = small[:, 4 * P + E + 1:4 * P + E + 2]
        router = sb("router", [P, 2 * E], F32R)
        bout = sb("bout", [P, D])
        ident = sb("ident", [P, P])
        head_mask = sb("head_mask", [P, P])
        iota = sb("iota", [P, E], U32)
        neg_half = sb("neg_half", [P, C])
        euler = sb("euler", [P, C])

        x_all = sb("x_all", [P, B, C, D])
        stats_all = sb("stats_all", [P, B, C, 6])
        mv_all = sb("mv_all", [P, B, C, 2])
        vareps_all = sb("vareps_all", [P, B, C])
        rstd_all = sb("rstd_all", [P, B, C])
        xhat = sb("xhat", [P, C, D])
        xnT = sb("xnT", [P, N])
        expT = sb("expT", [P, N])
        kneg = sb("kneg", [P, 1])
        ksum = sb("ksum", [P, 1])
        kinv = sb("kinv", [P, 1])
        probT = sb("probT", [P, N])
        prob = sb("prob", [P, C, P])
        av = sb("av", [P, P])
        ctxm = sb("ctxm", [P, P])
        ctxo = sb("ctxo", [P, D])
        mix = sb("mix", [P, D])
        x_plus = sb("x_plus", [P, C, D])
        x_twice = sb("x_twice", [P, C, D])
        res = sb("res", [P, C, D])
        stats = sb("stats", [P, C, 6])
        mv = sb("mv", [P, C, 2])
        vareps = sb("vareps", [P, C])
        rstd = sb("rstd", [P, C])
        x1 = [sb(f"x1_{i}", [P, C, D]) for i in range(2)]
        x1_hi = [sb(f"x1_hi{i}", [P, N], F32R) for i in range(2)]
        x1_lo = [sb(f"x1_lo{i}", [P, N], F32R) for i in range(2)]

        logits = sb("logits", [P, C, E])
        logits_lo = sb("logits_lo", [P, C, E])
        top = sb("top", [P, C, 8])
        topi = sb("topi", [P, C, 8], U32)
        gap = sb("gap", [P, C])
        gap_exp = sb("gap_exp", [P, C])
        den = sb("den", [P, C])
        weights = sb("weights", [P, C, 2])
        chosen = sb("chosen", [P, C, 2, E])
        chosen_w = sb("chosen_w", [P, C, 2, E])
        comb = sb("comb", [P, C, E])
        combT = sb("combT", [C * E, P])
        gate = w_loaded_flat[:, 0:E * N].rearrange("p (e n) -> p e n", e=E)
        GATE_SPAN = -(-E * N // (3 * H))

        act_g = [sb(f"act_g{i}", [P, N]) for i in range(R)]
        hid = [sb(f"hid{i}", [P, N]) for i in range(R)]
        gated = [sb(f"gated{i}", [P, N]) for i in range(R)]
        h_hi = [sb(f"h_hi{i}", [P, N], F32R) for i in range(RH)]
        h_lo = [sb(f"h_lo{i}", [P, N], F32R) for i in range(RH)]

        yT = sb("yT", [P, N])
        res2 = sb("res2", [P, C, D])
        stats2 = sb("stats2", [P, C, 6])
        mv2 = sb("mv2", [P, C, 2])
        vareps2 = sb("vareps2", [P, C])
        rstd2 = sb("rstd2", [P, C])
        out_sb = sb("out_sb", [P, C, D])

        def bank(name):
            return ctx.enter_context(nc.psum_tensor(name, [P, N], F32))

        ps_g = [bank(f"ps_g{i}") for i in range(R)]
        ps_u = [bank(f"ps_u{i}") for i in range(R)]
        ps_y = bank("ps_y")
        ps_a = bank("ps_a")

        PARTS = 2
        CP = C // PARTS

        def part(q):
            return slice(q * CP * P, (q + 1) * CP * P)

        def chunks(q):
            return range(q * CP, (q + 1) * CP)

        def tail_bank(q):
            return ps_a if q == 0 else ps_g[0]

        spare = ps_u[R - 1]

        comb_dram = nc.dram_tensor("comb_dram", [B, C, E, P], F32, kind="Internal").ap()

        x_loaded = [sem(f"x_loaded{b}") for b in range(B)]
        small_loaded, bout_loaded = sem("small_loaded"), sem("bout_loaded")
        w_loaded = [sem(f"w_loaded{i}") for i in range(NX)]
        w_hi_done, w_lo_dve, w_lo_pool = sem("w_hi_done"), sem("w_lo_dve"), sem("w_lo_pool")
        router_hi_done, router_lo_done = sem("router_hi_done"), sem("router_lo_done")
        ident_zero, consts_done, mask_done = sem("ident_zero"), sem("consts_done"), sem("mask_done")
        mask_zero = sem("mask_zero")
        stats_all_done, mv_all_done = sem("stats_all_done"), sem("mv_all_done")
        vareps_all_done, rstd_all_done = sem("vareps_all_done"), sem("rstd_all_done")
        xhat_done, xhatT_done, xn_done = sem("xhat_done"), sem("xhatT_done"), sem("xn_done")
        k_done, kmax_done, exp_done = sem("k_done"), sem("kmax_done"), sem("exp_done")
        kinv_done, probT_done, probt_done = sem("kinv_done"), sem("probT_done"), sem("probt_done")
        prob_done, av_done, av_copied = sem("prob_done"), sem("av_done"), sem("av_copied")
        ctx_done, ctxm_done = sem("ctx_done"), sem("ctxm_done")
        ctxo_done, ctxo_copied = sem("ctxo_done"), sem("ctxo_copied")
        mix_done, mix_copied, attn_done = sem("mix_done"), sem("mix_copied"), sem("attn_done")
        x_plus_done, x_twice_done, res_done = sem("x_plus_done"), sem("x_twice_done"), sem("res_done")
        stats_done, mv_done = sem("stats_done"), sem("mv_done")
        vareps_done, rstd_done, x1_done = sem("vareps_done"), sem("rstd_done"), sem("x1_done")
        x1T_done, x1_hi_done, x1_lo_done = sem("x1T_done"), sem("x1_hi_done"), sem("x1_lo_done")
        logits_done, logits_copied = sem("logits_done"), sem("logits_copied")
        logits_lo_copied = sem("logits_lo_copied")
        top_done, gap_done, gap_exp_done = sem("top_done"), sem("gap_done"), sem("gap_exp_done")
        den_done, w0_done, weights_done = sem("den_done"), sem("w0_done"), sem("weights_done")
        topi_done, chosen_done, chosen_w_done = sem("topi_done"), sem("chosen_done"), sem("chosen_w_done")
        comb_done, combT_done, combT_copied = sem("comb_done"), sem("combT_done"), sem("combT_copied")
        comb_stored = sem("comb_stored")
        gate_loaded = [sem(f"gate_loaded{e}") for e in range(E)]
        g_done, u_done, silu_done = sem("g_done"), sem("u_done"), sem("silu_done")
        hid_done, gated_done = sem("hid_done"), sem("gated_done")
        h_hi_done, h_lo_done, down_done = sem("h_hi_done"), sem("h_lo_done"), sem("down_done")
        y_copied, y_turned, res2_done = sem("y_copied"), sem("y_turned"), sem("res2_done")
        stats2_done, mv2_done = sem("stats2_done"), sem("mv2_done")
        vareps2_done, rstd2_done = sem("vareps2_done"), sem("rstd2_done")
        out_ready, out_stored = sem("out_ready"), sem("out_stored")

        class Slots:
            DOWN = LAG + 2
            """After which half of a step the products of each stage come: of tile t + 1's attention
            and routing, and of tile t - 1's last norm (Y). The other engines take a stage's products
            at the start of the next half."""
            XT, K, Y, PROB, AV, CTX, CTXO, MIX, ATT, X1T, ROUTE, COMB = 0, 1, 4, 5, 6, 7, 8, 9, 10, 14, 15, 17

        class FirstSlots(Slots):
            XT = K = PROB = AV = -NH
            COMB0, CTX, CTXO, MIX, ATT, X1T, ROUTE, COMB = 1, 3, 5, 7, 8, 12, 13, 16
            DOWN = LAG
            STATS = 1, 7, 10, 11, 13

        def half_at(j, last):
            if last and j > 0:
                j = j + 1 if j < NH - 1 else HH - 1
            return j // HH, j % HH

        def gated_before(j, last):
            return max(j - HH, 0) if not last else max(min(j - 1, NG), 0)

        SPLITS_DVE, SPLITS_POOL = [0, 1, 6, 7, 8], [2, 3, 4, 5]

        def bcast(ap, shape):
            return ap.to_broadcast(shape)

        waited = {e: sem(f"waited_{n}") for e, n in ((nc.vector, "dve"), (nc.gpsimd, "pool"), (nc.sync, "sp"))}

        def wait_apart(eng, semaphore, value):
            eng.wait_ge(semaphore, value)
            if not isinstance(value, int):
                eng.sem_inc(waited[eng], 1)

        block = ctx.enter_context(nc.Block())

        def steps(eng, step):
            step(Tile(0, 0), True, False)
            with eng.Fori(0, (B - 2) // 2) as i:
                step(Tile(i * 2 + 1, 1), False, False)
                step(Tile(i * 2 + 2, 0), False, False)
            step(Tile(LAST, LAST % 2), False, True)

        @block.sync
        def _(sp):
            x_view = x_d.rearrange("b (c p) d -> b p c d", p=P)
            out_view = out_d.rearrange("b (c p) d -> b p c d", p=P)

            def load_x(b):
                sp.dma_start(x_all[:, b, :, :], x_view[b]).then_inc(x_loaded[b], 16)

            def load_expert(e):
                sp.dma_start(w_raw[:, e, :], experts_d[e]).then_inc(w_loaded[e], 16)

            load_x(0)
            sp.dma_start(small[:, :], small_d).then_inc(small_loaded, 16)
            load_expert(0)
            sp.dma_start(bout[:, :], bout_d.partition_broadcast(P)).then_inc(bout_loaded, 16)
            load_x(1)
            for e in range(1, 3):
                load_expert(e)
            load_x(2)
            for e in range(3, NX):
                load_expert(e)
            for b in range(3, B):
                load_x(b)

            def spread_gates(a):
                wait_apart(sp, combT_copied, a.t + 1)
                sp.dma_start(comb_dram[a.t].rearrange("c e n -> (c e) n"), combT[:, :]).then_inc(comb_stored, 16)
                wait_apart(sp, comb_stored, a.t * 16 + 16)
                if isinstance(a.t, int) and a.t == 0:
                    sp.wait_ge(w_lo_dve, len([e for e in SPLITS_DVE if e < GATE_SPAN]))
                    sp.wait_ge(w_lo_pool, len([e for e in SPLITS_POOL if e < GATE_SPAN]))
                for e in range(E):
                    if not (isinstance(a.t, int) and a.t == 0):
                        sp.wait_ge(gated_done, (a.t - 1) * NG + HH * (e + 1))
                    sp.dma_start(gate[:, e, :].rearrange("p (c n) -> p c n", c=C),
                                 comb_dram[a.t, :, e, :].partition_broadcast(P))\
                      .then_inc(gate_loaded[e], 16)

            def store(t):
                wait_apart(sp, out_ready, t.t + 1)
                sp.dma_start(out_view[t.t], out_sb[:, :, :])\
                  .then_inc(out_stored, 16)

            def step(t, first, last):
                if first:
                    spread_gates(t)
                else:
                    store(t.prev())
                if not last:
                    spread_gates(t.next())

            steps(sp, step)
            for q in range(PARTS):
                sp.wait_ge(out_ready, B + q)
                sp.dma_start(out_view[LAST][:, q * CP:(q + 1) * CP, :], out_sb[:, q * CP:(q + 1) * CP, :])\
                  .then_inc(out_stored, 16)
            sp.wait_ge(out_stored, 16 * (LAST + PARTS))

        @block.gpsimd
        def _(pool):
            pool.memset(ident[:, :], 0.0).then_inc(ident_zero, 1)
            pool.memset(neg_half[:, :], -0.5)
            pool.memset(euler[:, :], 2.718281828459045)
            pool.iota(iota[:, :], pattern=[[1, E]], base=0, channel_multiplier=0)
            pool.wait_ge(ident_zero, 1)
            pool.affine_select(out=ident[:, :], in_=ident[:, :], compare_op=ALU.not_equal, fill=1.0,
                               base=0, pattern=[[-1, P]], channel_multiplier=1).then_inc(consts_done, 1)
            pool.wait_ge(consts_done, 1)

            def inverse_root(out, var, tmp, var_ready, n, tmp_done, done):
                wait_apart(pool, var_ready, n)
                pool.tensor_scalar(tmp, var, EPS, None, ALU.add).then_inc(tmp_done, 1)
                pool.wait_ge(tmp_done, n)
                pool.tensor_tensor(out, tmp, neg_half[:, 0:out.shape[1]], ALU.pow).then_inc(done, 1)

            def twice_x(a):
                if isinstance(a.t, int) and a.t < 2:
                    pool.wait_ge(x_loaded[a.t], 16)
                    pool.wait_ge(bout_loaded, 16)
                if not (isinstance(a.t, int) and a.t == 0):
                    wait_apart(pool, res_done, a.t)
                pool.tensor_tensor(x_plus[:, :, :], x_all[:, a.t, :, :],
                                   bout[:, None, :].to_broadcast([P, C, D]), ALU.add).then_inc(x_plus_done, 1)
                wait_apart(pool, x_plus_done, a.t + 1)
                pool.tensor_tensor(x_twice[:, :, :], x_plus[:, :, :], x_all[:, a.t, :, :], ALU.add)\
                    .then_inc(x_twice_done, 1)

            def norm_x(b):
                inverse_root(rstd_all[:, b, :], mv_all[:, b, :, 1], vareps_all[:, b, :],
                             mv_all_done, b + 1, vareps_all_done, rstd_all_done)

            def split_weights(e):
                pool.wait_ge(w_hi_done, e + 1)
                pool.tensor_tensor(w_lo[:, e, :], w_raw[:, e, :], w_hi[:, e, :].bitcast(F32), ALU.subtract)\
                    .then_inc(w_lo_pool, 1)

            def norm1(a):
                inverse_root(rstd[:, :], mv[:, :, 1], vareps[:, :], mv_done, a.t + 1, vareps_done, rstd_done)

            def gap_power(a):
                pool.wait_ge(gap_done, a.t + 1)
                pool.tensor_tensor(gap_exp[:, :], euler[:, :], gap[:, :], ALU.pow).then_inc(gap_exp_done, 1)

            def norm2(t):
                inverse_root(rstd2[:, :], mv2[:, :, 1], vareps2[:, :], mv2_done, t.t + 1, vareps2_done, rstd2_done)

            norm_x(0)
            twice_x(Tile(0, 0))
            norm_x(1)
            for e in SPLITS_POOL:
                split_weights(e)
                if e == SPLITS_POOL[0]:
                    norm_x(2)
            norm1(Tile(0, 0))
            gap_power(Tile(0, 0))

            def gate_half(t, j, last):
                e, h = half_at(j, last)
                if e == 0:
                    return
                e -= 1
                n = t.t * NH + j
                if h == 0:
                    pool.wait_ge(gate_loaded[e], t.t * 16 + 16)
                pool.wait_ge(hid_done, n + 1)
                if not (isinstance(n, int) and n < R):
                    pool.wait_ge(h_lo_done, n - R + 1)
                pool.tensor_tensor(gated[j % R][:, :], hid[j % R][:, :], gate[:, e, :], ALU.mult)\
                    .then_inc(gated_done, 1)

            def step(t, first, last):
                a = None if last else t.next()
                S = FirstSlots if first else Slots
                for j in range(NH):
                    if first and j - 1 in S.STATS:
                        norm_x(3 + S.STATS.index(j - 1))
                    gate_half(t, j, last)
                    if not last:
                        if j == 1:
                            twice_x(a)
                        if j == S.ATT + 2:
                            norm1(a)
                        if j == S.ROUTE:
                            gap_power(a)
                    if not first and j == S.Y + 4:
                        norm2(t.prev())

            steps(pool, step)
            for q in range(PARTS):
                c = slice(q * CP, (q + 1) * CP)
                inverse_root(rstd2[:, c], mv2[:, c, 1], vareps2[:, c], mv2_done, B + q, vareps2_done, rstd2_done)

        @block.scalar
        def _(act):
            act.wait_ge(small_loaded, 16)
            act.activation(router[:, 0:E], router_raw, ACT.Copy).then_inc(router_hi_done, 1)

            def split_weights(e):
                act.wait_ge(w_loaded[e], 16)
                act.activation(w_hi[:, e, :], w_raw[:, e, :], ACT.Copy).then_inc(w_hi_done, 1)

            def norm_out(a, bank=ps_a):
                act.wait_ge(xhatT_done, a.t + 1)
                act.activation(xnT[:, :], bank[:, :], ACT.Identity, bias=beta, scale=gamma)\
                   .then_inc(xn_done, 1)

            def exps(a, bank=ps_a):
                act.wait_ge(kmax_done, a.t + 1)
                act.activation(expT[:, :], bank[:, :], ACT.Exp, bias=kneg[:, :], accum_out=ksum[:, :])\
                   .then_inc(exp_done, 1)

            def copy(a, dst, src, ready, done):
                act.wait_ge(ready, a.t + 1)
                act.activation(dst, src, ACT.Copy).then_inc(done, 1)

            def copy_prob(a, bank=ps_a):
                copy(a, prob[:, :, :].rearrange("p c d -> p (c d)"), bank[:, :], probt_done, prob_done)

            def copy_ctxo(a):
                copy(a, ctxo[:, :], ps_a[:, 0:D], ctxo_done, ctxo_copied)

            def copy_mix(a):
                copy(a, mix[:, :], ps_a[:, 0:D], mix_done, mix_copied)

            def x1_high(a):
                copy(a, x1_hi[a.p][:, :], ps_a[:, :], x1T_done, x1_hi_done)

            def copy_combT(a):
                if not (isinstance(a.t, int) and a.t == 0):
                    act.wait_ge(comb_stored, a.t * 16)
                copy(a, combT[:, :], ps_a[0:C * E, 0:P], combT_done, combT_copied)

            zero, one = Tile(0, 0), Tile(1, 1)
            norm_out(zero)
            split_weights(0)
            exps(zero)
            split_weights(1)
            split_weights(2)
            copy_prob(zero)
            split_weights(3)
            split_weights(4)
            split_weights(5)
            split_weights(6)
            copy_ctxo(zero)
            copy_mix(zero)
            split_weights(7)
            norm_out(one, spare)
            split_weights(8)
            exps(one, spare)
            x1_high(zero)
            copy_prob(one, spare)

            def silu(t, j):
                n = t.t * NH + j
                act.wait_ge(g_done, n + 1)
                if not (isinstance(n, int) and n < R):
                    act.wait_ge(hid_done, n - R + 1)
                act.activation(act_g[j % R][:, :], ps_g[j % R][:, :], ACT.Silu).then_inc(silu_done, 1)

            def high(t, j, last=False):
                n = t.t * NH + j
                if half_at(j, last)[0] == 0:
                    act.wait_ge(hid_done, n + 1)
                else:
                    act.wait_ge(gated_done, t.t * NG + gated_before(j, last) + 1)
                if not (isinstance(n, int) and n < RH):
                    act.wait_ge(down_done, n - RH + 1)
                act.activation(h_hi[j % RH][:, :], gated[j % R][:, :], ACT.Copy).then_inc(h_hi_done, 1)

            def step(t, first, last):
                a = None if last else t.next()
                S = FirstSlots if first else Slots
                for j in range(NH):
                    if not last:
                        if j == S.XT + 1:
                            norm_out(a)
                        if j == S.PROB + 1:
                            copy_prob(a)
                        if j == S.X1T + 1:
                            x1_high(a)
                    silu(t, j)
                    if first and j == S.COMB0:
                        copy_combT(t)
                    if not last:
                        if j == S.CTXO + 1:
                            copy_ctxo(a)
                        if j == S.MIX + 1:
                            copy_mix(a)
                    if j > 0:
                        high(t, j - 1, last)
                    elif not first:
                        high(t.prev(), NH - 1)
                    if not last and j == S.K + 1:
                        exps(a)
                if not last:
                    copy_combT(a)

            steps(act, step)
            end = Tile(LAST, 1)
            high(end, NH - 1, True)
            for q in range(PARTS):
                act.wait_ge(down_done, B * NH)
                act.activation(yT[:, part(q)], ps_y[:, part(q)], ACT.Copy).then_inc(y_copied, 1)

        @block.vector
        def _(dve):
            dve.memset(head_mask[:, :], 0.0).then_inc(mask_zero, 1)
            dve.wait_ge(mask_zero, 1)
            for h in range(HEADS):
                s = slice(h * DH, (h + 1) * DH)
                last = dve.memset(head_mask[s, s], DH ** -0.5)
            last.then_inc(mask_done, 1)

            def chunk_stats(x, st, ready, value, st_done):
                dve.wait_ge(ready, value)
                for c in range(st.shape[1]):
                    last = dve.bn_stats(st[:, c, :], x[:, c, :])
                last.then_inc(st_done, 1)

            def chunk_means(st, m, n, st_done, m_done):
                wait_apart(dve, st_done, n)
                for c in range(m.shape[1]):
                    last = dve.bn_aggr(m[:, c, :], st[:, c, :])
                last.then_inc(m_done, 1)

            def normalise(a):
                dve.wait_ge(rstd_all_done, a.t + 1 if isinstance(a.t, int) and a.t < 2 else B)
                for c in range(C):
                    dve.tensor_scalar(xhat[:, c, :], x_all[:, a.t, c, :], mv_all[:, a.t, c, 0:1],
                                      rstd_all[:, a.t, c:c + 1], ALU.subtract, ALU.mult).then_inc(xhat_done, 1)

            def key_max(a, bank=ps_a):
                dve.wait_ge(k_done, a.t + 1)
                dve.tensor_reduce(kneg[:, :], bank[:, :], AX.X, ALU.max, negate=True).then_inc(kmax_done, 1)

            def probabilities(a):
                dve.wait_ge(exp_done, a.t + 1)
                dve.reciprocal(kinv[:, :], ksum[:, :]).then_inc(kinv_done, 1)
                dve.wait_ge(kinv_done, a.t + 1)
                dve.tensor_scalar(probT[:, :], expT[:, :], kinv[:, :], None, ALU.mult).then_inc(probT_done, 1)

            def copy_av(a, bank=ps_a):
                dve.wait_ge(av_done, a.t + 1)
                dve.tensor_scalar(av[:, :], bank[:, 0:P], gamma, beta, ALU.mult, ALU.add)\
                   .then_inc(av_copied, 1)

            def mask_heads(a):
                dve.wait_ge(ctx_done, a.t + 1)
                dve.tensor_tensor(ctxm[:, :], ps_a[:, 0:P], head_mask[:, :], ALU.mult).then_inc(ctxm_done, 1)

            def residual(a):
                dve.wait_ge(attn_done, a.t + 1)
                dve.wait_ge(x_twice_done, a.t + 1)
                dve.tensor_tensor(res[:, :, :].rearrange("p c d -> p (c d)"), ps_a[:, :],
                                  x_twice[:, :, :].rearrange("p c d -> p (c d)"), ALU.add).then_inc(res_done, 1)

            def first_stats(a):
                chunk_stats(res, stats, res_done, a.t + 1, stats_done)

            def first_means(a):
                chunk_means(stats, mv, a.t + 1, stats_done, mv_done)

            def first_norm(a):
                dve.wait_ge(rstd_done, a.t + 1)
                for c in range(C):
                    dve.tensor_scalar(x1[a.p][:, c, :], res[:, c, :], mv[:, c, 0:1], rstd[:, c:c + 1],
                                      ALU.subtract, ALU.mult).then_inc(x1_done, 1)

            def x1_low(a):
                dve.wait_ge(x1_hi_done, a.t + 1)
                dve.tensor_tensor(x1_lo[a.p][:, :], ps_a[:, :], x1_hi[a.p][:, :].bitcast(F32), ALU.subtract)\
                   .then_inc(x1_lo_done, 1)

            def best_two(a):
                dve.wait_ge(logits_done, a.t + 1)
                parts = ps_a[:, 0:C * 2 * E].rearrange("p (c two e) -> p c two e", c=C, two=2)
                dve.tensor_copy(logits_lo[:, :, :], parts[:, :, 1, :]).then_inc(logits_lo_copied, 1)
                dve.wait_ge(logits_lo_copied, a.t + 1)
                dve.tensor_tensor(logits[:, :, :], parts[:, :, 0, :], logits_lo[:, :, :], ALU.add)\
                   .then_inc(logits_copied, 1)
                wait_apart(dve, logits_copied, a.t + 1)
                for c in range(C):
                    last = dve.max(top[:, c, :], logits[:, c, :])
                last.then_inc(top_done, 1)
                dve.wait_ge(top_done, a.t + 1)
                dve.tensor_tensor(gap[:, :], top[:, :, 1], top[:, :, 0], ALU.subtract).then_inc(gap_done, 1)

            def mark_two(a):
                for c in range(C):
                    last = dve.max_index(topi[:, c, :], top[:, c, :], logits[:, c, :])
                last.then_inc(topi_done, 1)
                dve.wait_ge(topi_done, a.t + 1)
                dve.tensor_tensor(chosen[:, :, :, :], iota[:, None, None, :].to_broadcast([P, C, 2, E]),
                                  topi[:, :, 0:2, None].to_broadcast([P, C, 2, E]), ALU.is_equal)\
                   .then_inc(chosen_done, 1)

            def combine_weights(a):
                dve.wait_ge(gap_exp_done, a.t + 1)
                dve.tensor_scalar(den[:, :], gap_exp[:, :], 1.0, None, ALU.add).then_inc(den_done, 1)
                dve.wait_ge(den_done, a.t + 1)
                dve.reciprocal(weights[:, :, 0], den[:, :]).then_inc(w0_done, 1)
                dve.wait_ge(w0_done, a.t + 1)
                dve.tensor_tensor(weights[:, :, 1], gap_exp[:, :], weights[:, :, 0], ALU.mult)\
                   .then_inc(weights_done, 1)
                dve.wait_ge(weights_done, a.t + 1)
                dve.wait_ge(chosen_done, a.t + 1)
                dve.tensor_tensor(chosen_w[:, :, :, :], chosen[:, :, :, :],
                                  weights[:, :, :, None].to_broadcast([P, C, 2, E]), ALU.mult)\
                   .then_inc(chosen_w_done, 1)
                dve.wait_ge(chosen_w_done, a.t + 1)
                dve.tensor_tensor(comb[:, :, :], chosen_w[:, :, 0, :], chosen_w[:, :, 1, :], ALU.add)\
                   .then_inc(comb_done, 1)

            def copy_y(t):
                dve.wait_ge(down_done, t.t * NH + NH)
                dve.tensor_copy(yT[:, :], ps_y[:, :]).then_inc(y_copied, 1)

            def last_residual(t):
                dve.wait_ge(y_turned, t.t + 1)
                dve.tensor_tensor(res2[:, :, :].rearrange("p c d -> p (c d)"), ps_y[:, :],
                                  x1[t.p][:, :, :].rearrange("p c d -> p (c d)"), ALU.add).then_inc(res2_done, 1)

            def last_stats(t):
                chunk_stats(res2, stats2, res2_done, t.t + 1, stats2_done)

            def last_means(t):
                chunk_means(stats2, mv2, t.t + 1, stats2_done, mv2_done)

            def last_norm(t):
                dve.wait_ge(rstd2_done, t.t + 1)
                if not (isinstance(t.t, int) and t.t == 0):
                    dve.wait_ge(out_stored, t.t * 16)
                for c in range(C):
                    last = dve.tensor_scalar(out_sb[:, c, :], res2[:, c, :], mv2[:, c, 0:1], rstd2[:, c:c + 1],
                                             ALU.subtract, ALU.mult)
                last.then_inc(out_ready, 1)

            def split_weights(e):
                dve.wait_ge(w_hi_done, e + 1)
                dve.tensor_tensor(w_lo[:, e, :], w_raw[:, e, :], w_hi[:, e, :].bitcast(F32), ALU.subtract)\
                   .then_inc(w_lo_dve, 1)

            def stats_x(b):
                chunk_stats(x_all[:, b, :, :], stats_all[:, b, :, :], x_loaded[b], 16, stats_all_done)
                chunk_means(stats_all[:, b, :, :], mv_all[:, b, :, :], b + 1, stats_all_done, mv_all_done)

            zero, one = Tile(0, 0), Tile(1, 1)
            stats_x(0)
            dve.wait_ge(router_hi_done, 1)
            dve.tensor_tensor(router[:, E:], router_raw, router[:, 0:E].bitcast(F32), ALU.subtract)\
               .then_inc(router_lo_done, 1)
            normalise(zero)
            stats_x(1)
            key_max(zero)
            split_weights(0)
            probabilities(zero)
            split_weights(1)
            stats_x(2)
            copy_av(zero)
            mask_heads(zero)
            normalise(one)
            split_weights(6)
            residual(zero)
            first_stats(zero)
            first_means(zero)
            key_max(one, spare)
            first_norm(zero)
            probabilities(one)
            x1_low(zero)
            split_weights(7)
            best_two(zero)
            mark_two(zero)
            copy_av(one, spare)
            combine_weights(zero)

            def product(t, j, last):
                n = t.t * NH + j
                dve.wait_ge(silu_done, n + 1)
                dve.wait_ge(u_done, n + 1)
                if not (isinstance(n, int) and n < R):
                    dve.wait_ge(h_lo_done, n - R + 1)
                dst = gated if half_at(j, last)[0] == 0 else hid
                dve.tensor_tensor(dst[j % R][:, :], ps_u[j % R][:, :], act_g[j % R][:, :], ALU.mult)\
                   .then_inc(hid_done, 1)

            def low(t, j):
                n = t.t * NH + j
                dve.wait_ge(h_hi_done, n + 1)
                dve.tensor_tensor(h_lo[j % RH][:, :], gated[j % R][:, :], h_hi[j % RH][:, :].bitcast(F32),
                                  ALU.subtract).then_inc(h_lo_done, 1)

            def step(t, first, last):
                a = None if last else t.next()
                S = FirstSlots if first else Slots
                for j in range(NH):
                    if first:
                        pass
                    elif j == S.Y + 1:
                        last_residual(t.prev())
                    if not last:
                        if j == S.XT:
                            normalise(a)
                        if j == S.K + 1:
                            key_max(a)
                        if j == S.K + 3:
                            probabilities(a)
                        if j == S.AV + 1:
                            copy_av(a)
                        if j == S.CTX + 1:
                            mask_heads(a)
                        if j == S.ATT + 1:
                            residual(a)
                        if j == S.ATT + 2:
                            first_stats(a)
                        if j == S.X1T:
                            first_norm(a)
                        if j == S.X1T + 1:
                            x1_low(a)
                        if j == S.ROUTE + 1:
                            best_two(a)
                        if j == S.COMB:
                            combine_weights(a)
                    if j >= 2:
                        low(t, j - 2)
                    elif not first:
                        low(t.prev(), NH - 2 + j)
                    if not first and j == LAG - 1:
                        copy_y(t.prev())
                    product(t, j, last)
                    if not last:
                        if j == S.ATT + 2:
                            first_means(a)
                        if j == S.ROUTE + 1:
                            mark_two(a)
                    if first:
                        if j == 2:
                            split_weights(SPLITS_DVE[-1])
                        if j in S.STATS:
                            stats_x(3 + S.STATS.index(j))
                    else:
                        if j == S.Y + 2:
                            last_stats(t.prev())
                        if j == S.Y + 3:
                            last_means(t.prev())
                        if j == S.Y + 6:
                            last_norm(t.prev())

            steps(dve, step)
            low(Tile(LAST, 1), NH - 2)
            low(Tile(LAST, 1), NH - 1)

            def tail_stats(q):
                c = slice(q * CP, (q + 1) * CP)
                dve.wait_ge(y_turned, B + q)
                dve.tensor_tensor(res2[:, c, :].rearrange("p c d -> p (c d)"), tail_bank(q)[:, part(q)],
                                  x1[LAST % 2][:, c, :].rearrange("p c d -> p (c d)"), ALU.add).then_inc(res2_done, 1)
                chunk_stats(res2[:, c, :], stats2[:, c, :], res2_done, B + q, stats2_done)
                chunk_means(stats2[:, c, :], mv2[:, c, :], B + q, stats2_done, mv2_done)

            def tail_norm(q):
                dve.wait_ge(rstd2_done, B + q)
                if q == 0:
                    dve.wait_ge(out_stored, 16 * LAST)
                for c in chunks(q):
                    last = dve.tensor_scalar(out_sb[:, c, :], res2[:, c, :], mv2[:, c, 0:1], rstd2[:, c:c + 1],
                                             ALU.subtract, ALU.mult)
                last.then_inc(out_ready, 1)

            for q in range(PARTS):
                tail_stats(q)
            for q in range(PARTS):
                tail_norm(q)

        @block.tensor
        def _(pe):
            def turn(dst, src, ready=None, count=0):
                for c in range(C):
                    if ready:
                        pe.wait_ge(ready, count + c + 1)
                    last = pe.transpose(dst[:, c * P:(c + 1) * P], src(c), ident[:, :])
                return last

            def turn_x(a, bank=ps_a):
                if not (isinstance(a.t, int) and a.t < 2):
                    pe.wait_ge(combT_copied, a.t)
                turn(bank, lambda c: xhat[:, c, :], xhat_done, a.t * C).then_inc(xhatT_done, 1)

            def keys(a, bank=ps_a):
                pe.wait_ge(xn_done, a.t + 1)
                pe.matmul(bank[:, :], wk, xnT[:, :], start=True, stop=True).then_inc(k_done, 1)

            def turn_prob(a, bank=ps_a):
                pe.wait_ge(probT_done, a.t + 1)
                turn(bank, lambda c: probT[:, c * P:(c + 1) * P]).then_inc(probt_done, 1)

            def weigh_x(a, bank=ps_a):
                pe.wait_ge(prob_done, a.t + 1)
                for c in range(C):
                    last = pe.matmul(bank[:, 0:P], xhat[:, c, :], prob[:, c, :], start=c == 0, stop=c == C - 1)
                last.then_inc(av_done, 1)

            def context(a):
                pe.wait_ge(av_copied, a.t + 1)
                if isinstance(a.t, int) and a.t == 1:
                    pe.wait_ge(combT_copied, 1)
                pe.matmul(ps_a[:, 0:P], wv, av[:, :], start=True, stop=True).then_inc(ctx_done, 1)

            def context_out(a):
                pe.wait_ge(ctxm_done, a.t + 1)
                pe.matmul(ps_a[:, 0:D], ctxm[:, :], wout, start=True, stop=True).then_inc(ctxo_done, 1)

            def mix_queries(a):
                pe.wait_ge(ctxo_copied, a.t + 1)
                pe.matmul(ps_a[:, 0:D], wqT, ctxo[:, :], start=True, stop=True).then_inc(mix_done, 1)

            def attend(a):
                pe.wait_ge(mix_copied, a.t + 1)
                for c in range(C):
                    last = pe.matmul(ps_a[:, c * D:(c + 1) * D], xnT[:, c * P:(c + 1) * P], mix[:, :],
                                     start=True, stop=True)
                last.then_inc(attn_done, 1)

            def turn_x1(a):
                turn(ps_a, lambda c: x1[a.p][:, c, :], x1_done, a.t * C).then_inc(x1T_done, 1)

            def route(a):
                pe.wait_ge(x1_lo_done, a.t + 1)
                for c in range(C):
                    n, at = slice(c * P, (c + 1) * P), c * 2 * E
                    pe.matmul(ps_a[:, at:at + 2 * E], x1_hi[a.p][:, n], router[:, :],
                              start=True, stop=False, skip_group_check=True)
                    last = pe.matmul(ps_a[:, at:at + E], x1_lo[a.p][:, n], router[:, 0:E],
                                     start=False, stop=True, skip_group_check=True)
                last.then_inc(logits_done, 1)

            def turn_comb(a):
                pe.wait_ge(comb_done, a.t + 1)
                pe.transpose(ps_a[0:C * E, 0:P], comb[:, :, :].rearrange("p c e -> p (c e)"), ident[:, :])\
                    .then_inc(combT_done, 1)

            def turn_y(t):
                pe.wait_ge(y_copied, t.t + 1)
                turn(ps_y, lambda c: yT[:, c * P:(c + 1) * P]).then_inc(y_turned, 1)

            def three(dst, e, col, hi, lo, start, stop):
                w = slice(col, col + P)
                pe.matmul(dst, w_hi[:, e, w], hi, start=start, stop=False)
                pe.matmul(dst, w_hi[:, e, w], lo, start=False, stop=False)
                return pe.matmul(dst, w_lo[:, e, w], hi, start=False, stop=stop)

            def up(t, j, first, last):
                e, h = half_at(j, last)
                n = t.t * NH + j
                if j == 0:
                    pe.wait_ge(x1_lo_done, t.t + 1)
                if first and h == 0:
                    if e in SPLITS_DVE:
                        pe.wait_ge(w_lo_dve, SPLITS_DVE.index(e) + 1)
                    else:
                        pe.wait_ge(w_lo_pool, SPLITS_POOL.index(e) + 1)
                free = not (isinstance(n, int) and n < R)
                if free:
                    pe.wait_ge(silu_done, n - R + 1)
                three(ps_g[j % R][:, :], e, h * P, x1_hi[t.p][:, :], x1_lo[t.p][:, :], True, True)\
                    .then_inc(g_done, 1)
                if free:
                    pe.wait_ge(hid_done, n - R + 1)
                elif ps_u[j] is spare:
                    pe.wait_ge(av_copied, 2)
                three(ps_u[j % R][:, :], e, H + h * P, x1_hi[t.p][:, :], x1_lo[t.p][:, :], True, True)\
                    .then_inc(u_done, 1)

            def down(t, j, last=False):
                e, h = half_at(j, last)
                pe.wait_ge(h_lo_done, t.t * NH + j + 1)
                if j == 0 and not (isinstance(t.t, int) and t.t == 0):
                    pe.wait_ge(res2_done, t.t)
                three(ps_y[:, :], e, WD + h * P, h_hi[j % RH][:, :], h_lo[j % RH][:, :], j == 0, j == NH - 1)\
                    .then_inc(down_done, 1)

            def keep_clock(n):
                for _ in range(n):
                    pe.matmul(ps_y[:, 0:P], ident[:, :], ident[:, :], start=True, stop=True)

            zero, one = Tile(0, 0), Tile(1, 1)
            pe.wait_ge(consts_done, 1)
            keep_clock(11)
            turn_x(zero)
            pe.wait_ge(small_loaded, 16)
            keep_clock(3)
            keys(zero)
            keep_clock(9)
            turn_prob(zero)
            keep_clock(3)
            weigh_x(zero)
            keep_clock(3)
            context(zero)
            keep_clock(2)
            context_out(zero)
            keep_clock(3)
            mix_queries(zero)
            keep_clock(3)
            attend(zero)
            turn_x(one, spare)
            keep_clock(3)
            keys(one, spare)
            keep_clock(6)
            turn_x1(zero)
            turn_prob(one, spare)
            keep_clock(3)
            pe.wait_ge(router_lo_done, 1)
            route(zero)
            weigh_x(one, spare)

            def step(t, first, last):
                a = None if last else t.next()
                S = FirstSlots if first else Slots
                for j in range(NH):
                    up(t, j, first, last)
                    if j >= S.DOWN:
                        for i in range(0 if j == S.DOWN else j - LAG, j - LAG + 1):
                            down(t, i, last)
                    elif j < LAG and not first:
                        down(t.prev(), NH - LAG + j)
                    if first:
                        if j == S.COMB0:
                            turn_comb(t)
                    if not first and j == S.Y:
                        turn_y(t.prev())
                    if not last:
                        if j == S.XT:
                            turn_x(a)
                        if j == S.K:
                            keys(a)
                        if j == S.PROB:
                            turn_prob(a)
                        if j == S.AV:
                            weigh_x(a)
                        if j == S.CTX:
                            context(a)
                        if j == S.CTXO:
                            context_out(a)
                        if j == S.MIX:
                            mix_queries(a)
                        if j == S.ATT:
                            attend(a)
                        if j == S.X1T:
                            turn_x1(a)
                        if j == S.ROUTE:
                            route(a)
                        if j == S.COMB:
                            turn_comb(a)

            steps(pe, step)
            end = Tile(LAST, 1)
            for j in range(NH - LAG, NH):
                down(end, j, True)
            for q in range(PARTS):
                pe.wait_ge(y_copied, B + q)
                for c in chunks(q):
                    last = pe.transpose(tail_bank(q)[:, c * P:(c + 1) * P], yT[:, c * P:(c + 1) * P], ident[:, :])
                last.then_inc(y_turned, 1)


def kernel(**inputs):
    import numpy as np
    import concourse.bacc as bacc
    from concourse import mybir as mb
    from concourse.bass_utils import run_bass_kernel_spmd

    a = {k: np.asarray(v) for k, v in inputs.items()}
    D = a["L0_attn_x"].shape[2]
    hidden = a["L0_attn_w_qkv"].shape[1] // 3
    w = a["L0_attn_w_qkv"]

    def up(m):
        return np.swapaxes(m, -1, -2)

    def down(m):
        m = np.swapaxes(m, -1, -2)
        m = m.reshape(*m.shape[:-2], m.shape[-2] // 128, 128, D)
        m = np.swapaxes(m, -3, -2)
        return m.reshape(*m.shape[:-2], -1)

    shared = np.concatenate([up(a["L0_ffn_sg"]), up(a["L0_ffn_su"]), down(a["L0_ffn_sd"])], axis=-1)
    routed = np.concatenate([up(a["L0_ffn_Wg"]), up(a["L0_ffn_Wu"]), down(a["L0_ffn_Wd"])], axis=-1)
    small = [w[:, hidden:2 * hidden], w[:, 2 * hidden:], a["L0_attn_w_out"], w[:, 0:hidden].T,
             a["L0_ffn_w_router"].T, a["L0_attn_gamma"].reshape(D, 1), a["L0_attn_beta"].reshape(D, 1)]
    arrays = {
        "x": a["L0_attn_x"],
        "small": np.concatenate(small, axis=1),
        "bout": a["L0_attn_b_out"],
        "experts": np.concatenate([shared[None], routed], axis=0),
    }
    arrays = {k + "_in": np.ascontiguousarray(v) for k, v in arrays.items()}
    nc = bacc.Bacc("TRN2", target_bir_lowering=False, num_devices=1)
    args = [nc.dram_tensor(k, v.shape, mb.dt.from_np(v.dtype), kind="ExternalInput").ap()
            for k, v in arrays.items()]
    out = nc.dram_tensor("out", a["L0_attn_x"].shape, mb.dt.float32, kind="ExternalOutput").ap()
    build(nc, *args, out)
    r = run_bass_kernel_spmd(nc, [arrays], core_ids=[0])
    return r.results[0]["out"]
```

```python
import concourse.bass as bass
from concourse import mybir
from contextlib import ExitStack



class Tile:

    def __init__(self, t, parity):
        self.t, self.p = t, parity

    def next(self):
        return Tile(self.t + 1, 1 - self.p)

    def prev(self):
        return Tile(self.t - 1, 1 - self.p)


def build(nc, x_d, small_d, bout_d, experts_d, out_d):
    F32, F32R, U32 = mybir.dt.float32, mybir.dt.float32r, mybir.dt.uint32
    ALU = mybir.AluOpType
    ACT = mybir.ActivationFunctionType
    AX = mybir.AxisListType

    B, N, D = x_d.shape
    P = 128
    C = N // P
    NX = experts_d.shape[0]
    E = NX - 1
    H = (experts_d.shape[2]) // 3
    HH = H // P
    NH = NX * HH
    NG = E * HH
    HEADS, DH = 4, 32
    EPS = 1e-5
    LAST = B - 1
    R = 3
    RH = 6
    LAG = 4
    WD = 2 * H

    ctx = ExitStack()
    with ctx:
        def sb(name, shape, dt=F32):
            return ctx.enter_context(nc.sbuf_tensor(name, shape, dt))

        def sem(name):
            return ctx.enter_context(nc.semaphore(name))

        w_hi = sb("w_hi", [P, NX, 3 * H], F32R)
        w_lo = sb("w_lo", [P, NX, 3 * H], F32R)
        w_raw_flat = sb("w_raw", [P, NX * 3 * H])
        w_raw = w_raw_flat[:, :].rearrange("p (e w) -> p e w", e=NX)
        small = sb("small", [P, 4 * P + E + 2])
        wk, wv, wout, wqT = (small[:, i * P:(i + 1) * P] for i in range(4))
        router_raw = small[:, 4 * P:4 * P + E]
        gamma = small[:, 4 * P + E:4 * P + E + 1]
        beta = small[:, 4 * P + E + 1:4 * P + E + 2]
        router = sb("router", [P, 2 * E], F32R)
        bout = sb("bout", [P, D])
        ident = sb("ident", [P, P])
        head_mask = sb("head_mask", [P, P])
        iota = sb("iota", [P, E], U32)
        neg_half = sb("neg_half", [P, C])
        euler = sb("euler", [P, C])

        x_all = sb("x_all", [P, B, C, D])
        stats_all = sb("stats_all", [P, B, C, 6])
        mv_all = sb("mv_all", [P, B, C, 2])
        vareps_all = sb("vareps_all", [P, B, C])
        rstd_all = sb("rstd_all", [P, B, C])
        xhat = sb("xhat", [P, C, D])
        xnT = sb("xnT", [P, N])
        expT = sb("expT", [P, N])
        kneg = sb("kneg", [P, 1])
        ksum = sb("ksum", [P, 1])
        kinv = sb("kinv", [P, 1])
        probT = sb("probT", [P, N])
        prob = sb("prob", [P, C, P])
        av = sb("av", [P, P])
        ctxm = sb("ctxm", [P, P])
        ctxo = sb("ctxo", [P, D])
        mix = sb("mix", [P, D])
        x_plus = sb("x_plus", [P, C, D])
        x_twice = sb("x_twice", [P, C, D])
        res = sb("res", [P, C, D])
        stats = sb("stats", [P, C, 6])
        mv = sb("mv", [P, C, 2])
        vareps = sb("vareps", [P, C])
        rstd = sb("rstd", [P, C])
        x1 = [sb(f"x1_{i}", [P, C, D]) for i in range(2)]
        x1_hi = [sb(f"x1_hi{i}", [P, N], F32R) for i in range(2)]
        x1_lo = [sb(f"x1_lo{i}", [P, N], F32R) for i in range(2)]

        logits = sb("logits", [P, C, E])
        logits_lo = sb("logits_lo", [P, C, E])
        top = sb("top", [P, C, 8])
        topi = sb("topi", [P, C, 8], U32)
        gap = sb("gap", [P, C])
        gap_exp = sb("gap_exp", [P, C])
        den = sb("den", [P, C])
        weights = sb("weights", [P, C, 2])
        chosen = sb("chosen", [P, C, 2, E])
        chosen_w = sb("chosen_w", [P, C, 2, E])
        comb = sb("comb", [P, C, E])
        combT = sb("combT", [C * E, P])
        gate = w_raw_flat[:, 0:E * N].rearrange("p (e n) -> p e n", e=E)
        GATE_SPAN = -(-E * N // (3 * H))

        act_g = [sb(f"act_g{i}", [P, N]) for i in range(R)]
        hid = [sb(f"hid{i}", [P, N]) for i in range(R)]
        gated = [sb(f"gated{i}", [P, N]) for i in range(R)]
        h_hi = [sb(f"h_hi{i}", [P, N], F32R) for i in range(RH)]
        h_lo = [sb(f"h_lo{i}", [P, N], F32R) for i in range(RH)]

        yT = sb("yT", [P, N])
        res2 = sb("res2", [P, C, D])
        stats2 = sb("stats2", [P, C, 6])
        mv2 = sb("mv2", [P, C, 2])
        vareps2 = sb("vareps2", [P, C])
        rstd2 = sb("rstd2", [P, C])
        out_sb = sb("out_sb", [P, C, D])

        def bank(name):
            return ctx.enter_context(nc.psum_tensor(name, [P, N], F32))

        ps_g = [bank(f"ps_g{i}") for i in range(R)]
        ps_u = [bank(f"ps_u{i}") for i in range(R)]
        ps_y = bank("ps_y")
        ps_a = bank("ps_a")

        spare_1 = ps_u[R - 1]
        spare_0 = ps_g[R - 1]

        comb_dram = nc.dram_tensor("comb_dram", [B, C, E, P], F32, kind="Internal").ap()

        x_loaded = [sem(f"x_loaded{b}") for b in range(B)]
        small_loaded, bout_loaded = sem("small_loaded"), sem("bout_loaded")
        w_loaded = [sem(f"w_loaded{i}") for i in range(NX)]
        w_hi_done, w_lo_dve, w_lo_pool = sem("w_hi_done"), sem("w_lo_dve"), sem("w_lo_pool")
        router_hi_done, router_lo_done = sem("router_hi_done"), sem("router_lo_done")
        ident_zero, consts_done, mask_done = sem("ident_zero"), sem("consts_done"), sem("mask_done")
        mask_zero = sem("mask_zero")
        stats_all_done, mv_all_done = sem("stats_all_done"), sem("mv_all_done")
        vareps_all_done, rstd_all_done = sem("vareps_all_done"), sem("rstd_all_done")
        xhat_done, xhatT_done, xn_done = sem("xhat_done"), sem("xhatT_done"), sem("xn_done")
        k_done, kmax_done, exp_done = sem("k_done"), sem("kmax_done"), sem("exp_done")
        kinv_done, probT_done, probt_done = sem("kinv_done"), sem("probT_done"), sem("probt_done")
        prob_done, av_done, av_copied = sem("prob_done"), sem("av_done"), sem("av_copied")
        ctx_done, ctxm_done = sem("ctx_done"), sem("ctxm_done")
        ctxo_done, ctxo_copied = sem("ctxo_done"), sem("ctxo_copied")
        mix_done, mix_copied, attn_done = sem("mix_done"), sem("mix_copied"), sem("attn_done")
        x_plus_done, x_twice_done, res_done = sem("x_plus_done"), sem("x_twice_done"), sem("res_done")
        stats_done, mv_done = sem("stats_done"), sem("mv_done")
        vareps_done, rstd_done, x1_done = sem("vareps_done"), sem("rstd_done"), sem("x1_done")
        x1T_done, x1_hi_done, x1_lo_done = sem("x1T_done"), sem("x1_hi_done"), sem("x1_lo_done")
        logits_done, logits_copied = sem("logits_done"), sem("logits_copied")
        logits_lo_copied = sem("logits_lo_copied")
        top_done, gap_done, gap_exp_done = sem("top_done"), sem("gap_done"), sem("gap_exp_done")
        den_done, w0_done, weights_done = sem("den_done"), sem("w0_done"), sem("weights_done")
        topi_done, chosen_done, chosen_w_done = sem("topi_done"), sem("chosen_done"), sem("chosen_w_done")
        comb_done, combT_done, combT_copied = sem("comb_done"), sem("combT_done"), sem("combT_copied")
        comb_stored = sem("comb_stored")
        gate_loaded = [sem(f"gate_loaded{e}") for e in range(E)]
        g_done, u_done, silu_done = sem("g_done"), sem("u_done"), sem("silu_done")
        hid_done, gated_done = sem("hid_done"), sem("gated_done")
        h_hi_done, h_lo_done, down_done = sem("h_hi_done"), sem("h_lo_done"), sem("down_done")
        y_copied, y_turned, res2_done = sem("y_copied"), sem("y_turned"), sem("res2_done")
        stats2_done, mv2_done = sem("stats2_done"), sem("mv2_done")
        vareps2_done, rstd2_done = sem("vareps2_done"), sem("rstd2_done")
        out_ready, out_stored = sem("out_ready"), sem("out_stored")

        class Part:
            early = {}

            def __init__(self, first, end):
                self.chunks, self.c, self.n = range(first, end), slice(first, end), slice(first * P, end * P)
                self.follows = end < C

            def of(self, s):
                if not self.follows:
                    return s
                if s.name not in self.early:
                    self.early[s.name] = sem("early_" + s.name)
                return self.early[s.name]

            def bank(self, other):
                return other if self.chunks[0] else ps_a

        WHOLE = Part(0, C)
        PARTS = Part(0, C // 2), Part(C // 2, C)

        class Slots:
            DOWN = LAG + 2
            XT, K, Y, PROB, AV, CTX, CTXO, MIX, ATT, X1T, ROUTE, COMB = 0, 1, 4, 5, 6, 7, 8, 9, 10, 14, 15, 17

        class FirstSlots(Slots):
            XT = K = PROB = AV = -NH
            COMB0, CTX, CTXO, MIX, ATT, X1T, ROUTE, COMB = 1, 3, 4, 6, 7, 11, 14, 17
            DOWN = LAG
            STATS = 1, 5, 9, 11, 13

        def half_at(j, last):
            if last and j > 0:
                j = j + 1 if j < NH - 1 else HH - 1
            return j // HH, j % HH

        def gated_before(j, last):
            return max(j - HH, 0) if not last else max(min(j - 1, NG), 0)

        SPLITS_DVE, SPLITS_POOL = [0, 1, 6, 7, 8], [2, 3, 4, 5]

        waited = {e: sem(f"waited_{n}") for e, n in ((nc.vector, "dve"), (nc.gpsimd, "pool"), (nc.sync, "sp"))}

        def wait_apart(eng, semaphore, value):
            eng.wait_ge(semaphore, value)
            if not isinstance(value, int):
                eng.sem_inc(waited[eng], 1)

        block = ctx.enter_context(nc.Block())

        def steps(eng, step):
            step(Tile(0, 0), True, False)
            with eng.Fori(0, (B - 2) // 2) as i:
                step(Tile(i * 2 + 1, 1), False, False)
                step(Tile(i * 2 + 2, 0), False, False)
            step(Tile(LAST, LAST % 2), False, True)

        @block.sync
        def _(sp):
            x_view = x_d.rearrange("b (c p) d -> b p c d", p=P)
            out_view = out_d.rearrange("b (c p) d -> b p c d", p=P)

            def load_x(b):
                sp.dma_start(x_all[:, b, :, :], x_view[b]).then_inc(x_loaded[b], 16)

            def load_expert(e):
                sp.dma_start(w_raw[:, e, :], experts_d[e]).then_inc(w_loaded[e], 16)

            load_x(0)
            sp.dma_start(small[:, :], small_d).then_inc(small_loaded, 16)
            load_expert(0)
            sp.dma_start(bout[:, :], bout_d.partition_broadcast(P)).then_inc(bout_loaded, 16)
            load_x(1)
            for e in range(1, 3):
                load_expert(e)
            load_x(2)
            for e in range(3, NX):
                load_expert(e)
            for b in range(3, B):
                load_x(b)

            def spread_gates(a):
                wait_apart(sp, combT_copied, a.t + 1)
                sp.dma_start(comb_dram[a.t].rearrange("c e n -> (c e) n"), combT[:, :]).then_inc(comb_stored, 16)
                wait_apart(sp, comb_stored, a.t * 16 + 16)
                if isinstance(a.t, int) and a.t == 0:
                    sp.wait_ge(w_lo_dve, len([e for e in SPLITS_DVE if e < GATE_SPAN]))
                    sp.wait_ge(w_lo_pool, len([e for e in SPLITS_POOL if e < GATE_SPAN]))
                for e in range(E):
                    if not (isinstance(a.t, int) and a.t == 0):
                        sp.wait_ge(gated_done, (a.t - 1) * NG + HH * (e + 1))
                    sp.dma_start(gate[:, e, :].rearrange("p (c n) -> p c n", c=C),
                                 comb_dram[a.t, :, e, :].partition_broadcast(P))\
                      .then_inc(gate_loaded[e], 16)

            def store(t):
                wait_apart(sp, out_ready, t.t + 1)
                sp.dma_start(out_view[t.t], out_sb[:, :, :])\
                  .then_inc(out_stored, 16)

            def step(t, first, last):
                if first:
                    spread_gates(t)
                else:
                    store(t.prev())
                if not last:
                    spread_gates(t.next())

            steps(sp, step)
            for q in PARTS:
                sp.wait_ge(q.of(out_ready), 1 if q.follows else B)
                sp.dma_start(out_view[LAST][:, q.c, :], out_sb[:, q.c, :]).then_inc(out_stored, 16)
            sp.wait_ge(out_stored, 16 * (LAST + len(PARTS)))

        @block.gpsimd
        def _(pool):
            pool.memset(ident[:, :], 0.0).then_inc(ident_zero, 1)
            pool.memset(neg_half[:, :], -0.5)
            pool.memset(euler[:, :], 2.718281828459045)
            pool.iota(iota[:, :], pattern=[[1, E]], base=0, channel_multiplier=0)
            pool.wait_ge(ident_zero, 1)
            pool.affine_select(out=ident[:, :], in_=ident[:, :], compare_op=ALU.not_equal, fill=1.0,
                               base=0, pattern=[[-1, P]], channel_multiplier=1).then_inc(consts_done, 1)
            pool.wait_ge(consts_done, 1)

            def inverse_root(out, var, tmp, var_ready, n, tmp_done, done, q=WHOLE):
                var_ready, tmp_done, done = q.of(var_ready), q.of(tmp_done), q.of(done)
                n = 1 if q.follows else n
                out, tmp, var = out[:, q.c], tmp[:, q.c], var[:, q.c]
                wait_apart(pool, var_ready, n)
                pool.tensor_scalar(tmp, var, EPS, None, ALU.add).then_inc(tmp_done, 1)
                pool.wait_ge(tmp_done, n)
                pool.tensor_tensor(out, tmp, neg_half[:, 0:out.shape[1]], ALU.pow).then_inc(done, 1)

            def twice_x(a):
                if isinstance(a.t, int) and a.t < 2:
                    pool.wait_ge(x_loaded[a.t], 16)
                    pool.wait_ge(bout_loaded, 16)
                if not (isinstance(a.t, int) and a.t == 0):
                    wait_apart(pool, res_done, a.t)
                pool.tensor_tensor(x_plus[:, :, :], x_all[:, a.t, :, :],
                                   bout[:, None, :].to_broadcast([P, C, D]), ALU.add).then_inc(x_plus_done, 1)
                wait_apart(pool, x_plus_done, a.t + 1)
                pool.tensor_tensor(x_twice[:, :, :], x_plus[:, :, :], x_all[:, a.t, :, :], ALU.add)\
                    .then_inc(x_twice_done, 1)

            def norm_x(b, q=WHOLE):
                inverse_root(rstd_all[:, b, :], mv_all[:, b, :, 1], vareps_all[:, b, :],
                             mv_all_done, b + 1, vareps_all_done, rstd_all_done, q)

            def split_weights(e):
                pool.wait_ge(w_hi_done, e + 1)
                pool.tensor_tensor(w_lo[:, e, :], w_raw[:, e, :], w_hi[:, e, :].bitcast(F32), ALU.subtract)\
                    .then_inc(w_lo_pool, 1)

            def norm1(a, q=WHOLE):
                inverse_root(rstd, mv[:, :, 1], vareps, mv_done, a.t + 1, vareps_done, rstd_done, q)

            def gap_power(a):
                pool.wait_ge(gap_done, a.t + 1)
                pool.tensor_tensor(gap_exp[:, :], euler[:, :], gap[:, :], ALU.pow).then_inc(gap_exp_done, 1)

            def norm2(t, q=WHOLE):
                inverse_root(rstd2, mv2[:, :, 1], vareps2, mv2_done, t.t + 1, vareps2_done, rstd2_done, q)

            for q in PARTS:
                norm_x(0, q)
            twice_x(Tile(0, 0))
            norm_x(1)
            split_weights(SPLITS_POOL[0])
            norm_x(2)
            for e in SPLITS_POOL[1:-1]:
                split_weights(e)
            for q in PARTS:
                norm1(Tile(0, 0), q)
            split_weights(SPLITS_POOL[-1])
            gap_power(Tile(0, 0))

            def gate_half(t, j, last):
                e, h = half_at(j, last)
                if e == 0:
                    return
                e -= 1
                n = t.t * NH + j
                if h == 0:
                    pool.wait_ge(gate_loaded[e], t.t * 16 + 16)
                pool.wait_ge(hid_done, n + 1)
                if not (isinstance(n, int) and n < R):
                    pool.wait_ge(h_lo_done, n - R + 1)
                pool.tensor_tensor(gated[j % R][:, :], hid[j % R][:, :], gate[:, e, :], ALU.mult)\
                    .then_inc(gated_done, 1)

            def step(t, first, last):
                a = None if last else t.next()
                S = FirstSlots if first else Slots
                for j in range(NH):
                    if first and j - 1 in S.STATS:
                        norm_x(3 + S.STATS.index(j - 1))
                    gate_half(t, j, last)
                    if not last:
                        if j == 1:
                            twice_x(a)
                        if j == S.ATT + 2:
                            norm1(a)
                        if j == S.ROUTE:
                            gap_power(a)
                    if not first and j == S.Y + 4:
                        norm2(t.prev())

            steps(pool, step)
            for q in PARTS:
                norm2(Tile(LAST, 1), q)

        @block.scalar
        def _(act):
            act.wait_ge(small_loaded, 16)
            act.activation(router[:, 0:E], router_raw, ACT.Copy).then_inc(router_hi_done, 1)

            def split_weights(e):
                act.wait_ge(w_loaded[e], 16)
                act.activation(w_hi[:, e, :], w_raw[:, e, :], ACT.Copy).then_inc(w_hi_done, 1)

            def norm_out(a, bank=ps_a):
                act.wait_ge(xhatT_done, a.t + 1)
                act.activation(xnT[:, :], bank[:, :], ACT.Identity, bias=beta, scale=gamma)\
                   .then_inc(xn_done, 1)

            def exps(a, bank=ps_a):
                act.wait_ge(kmax_done, a.t + 1)
                act.activation(expT[:, :], bank[:, :], ACT.Exp, bias=kneg[:, :], accum_out=ksum[:, :])\
                   .then_inc(exp_done, 1)

            def copy(a, dst, src, ready, done):
                act.wait_ge(ready, a.t + 1)
                act.activation(dst, src, ACT.Copy).then_inc(done, 1)

            def copy_prob(a, bank=ps_a):
                copy(a, prob[:, :, :].rearrange("p c d -> p (c d)"), bank[:, :], probt_done, prob_done)

            def copy_ctxo(a):
                copy(a, ctxo[:, :], ps_a[:, 0:D], ctxo_done, ctxo_copied)

            def copy_mix(a):
                copy(a, mix[:, :], ps_a[:, 0:D], mix_done, mix_copied)

            def x1_high(a, q=WHOLE):
                copy(a, x1_hi[a.p][:, q.n], q.bank(spare_0)[:, q.n], q.of(x1T_done), q.of(x1_hi_done))

            def copy_combT(a):
                if not (isinstance(a.t, int) and a.t == 0):
                    act.wait_ge(comb_stored, a.t * 16)
                copy(a, combT[:, :], ps_a[0:C * E, 0:P], combT_done, combT_copied)

            zero, one = Tile(0, 0), Tile(1, 1)
            norm_out(zero)
            split_weights(0)
            exps(zero)
            split_weights(1)
            split_weights(2)
            copy_prob(zero)
            split_weights(3)
            split_weights(4)
            split_weights(5)
            split_weights(6)
            copy_ctxo(zero)
            copy_mix(zero)
            split_weights(7)
            norm_out(one, spare_1)
            split_weights(8)
            exps(one, spare_1)
            for q in PARTS:
                x1_high(zero, q)
            copy_prob(one, spare_1)

            def silu(t, j):
                n = t.t * NH + j
                act.wait_ge(g_done, n + 1)
                if not (isinstance(n, int) and n < R):
                    act.wait_ge(hid_done, n - R + 1)
                act.activation(act_g[j % R][:, :], ps_g[j % R][:, :], ACT.Silu).then_inc(silu_done, 1)

            def high(t, j, last=False):
                n = t.t * NH + j
                if half_at(j, last)[0] == 0:
                    act.wait_ge(hid_done, n + 1)
                else:
                    act.wait_ge(gated_done, t.t * NG + gated_before(j, last) + 1)
                if not (isinstance(n, int) and n < RH):
                    act.wait_ge(down_done, n - RH + 1)
                act.activation(h_hi[j % RH][:, :], gated[j % R][:, :], ACT.Copy).then_inc(h_hi_done, 1)

            def step(t, first, last):
                a = None if last else t.next()
                S = FirstSlots if first else Slots
                for j in range(NH):
                    if not last:
                        if j == S.XT + 1:
                            norm_out(a)
                        if j == S.PROB + 1:
                            copy_prob(a)
                        if j == S.X1T + 1:
                            x1_high(a)
                    silu(t, j)
                    if first and j == S.COMB0:
                        copy_combT(t)
                    if not last:
                        if j == S.CTXO + 1:
                            copy_ctxo(a)
                        if j == S.MIX + 1:
                            copy_mix(a)
                    if j > 0:
                        high(t, j - 1, last)
                    elif not first:
                        high(t.prev(), NH - 1)
                    if not last and j == S.K + 1:
                        exps(a)
                if not last:
                    copy_combT(a)

            steps(act, step)
            end = Tile(LAST, 1)
            high(end, NH - 1, True)
            for q in PARTS:
                act.wait_ge(down_done, B * NH)
                act.activation(yT[:, q.n], ps_y[:, q.n], ACT.Copy).then_inc(q.of(y_copied), 1)

        @block.vector
        def _(dve):
            dve.memset(head_mask[:, :], 0.0).then_inc(mask_zero, 1)
            dve.wait_ge(mask_zero, 1)
            for h in range(HEADS):
                s = slice(h * DH, (h + 1) * DH)
                last = dve.memset(head_mask[s, s], DH ** -0.5)
            last.then_inc(mask_done, 1)
            dve.wait_ge(mask_done, 1)

            def chunk_stats(x, st, ready, value, st_done, q):
                dve.wait_ge(ready, value)
                for c in q.chunks:
                    last = dve.bn_stats(st[:, c, :], x[:, c, :])
                last.then_inc(q.of(st_done), 1)

            def chunk_means(st, m, n, st_done, m_done, q):
                wait_apart(dve, q.of(st_done), 1 if q.follows else n)
                for c in q.chunks:
                    last = dve.bn_aggr(m[:, c, :], st[:, c, :])
                last.then_inc(q.of(m_done), 1)

            def normalise(a, q=WHOLE):
                dve.wait_ge(q.of(rstd_all_done), a.t + 1 if isinstance(a.t, int) and a.t < 2 else B)
                for c in q.chunks:
                    dve.tensor_scalar(xhat[:, c, :], x_all[:, a.t, c, :], mv_all[:, a.t, c, 0:1],
                                      rstd_all[:, a.t, c:c + 1], ALU.subtract, ALU.mult).then_inc(xhat_done, 1)

            def key_max(a, bank=ps_a):
                dve.wait_ge(k_done, a.t + 1)
                dve.tensor_reduce(kneg[:, :], bank[:, :], AX.X, ALU.max, negate=True).then_inc(kmax_done, 1)

            def probabilities(a):
                dve.wait_ge(exp_done, a.t + 1)
                dve.reciprocal(kinv[:, :], ksum[:, :]).then_inc(kinv_done, 1)
                dve.wait_ge(kinv_done, a.t + 1)
                dve.tensor_scalar(probT[:, :], expT[:, :], kinv[:, :], None, ALU.mult).then_inc(probT_done, 1)

            def copy_av(a, bank=ps_a):
                dve.wait_ge(av_done, a.t + 1)
                dve.tensor_scalar(av[:, :], bank[:, 0:P], gamma, beta, ALU.mult, ALU.add)\
                   .then_inc(av_copied, 1)

            def mask_heads(a):
                dve.wait_ge(ctx_done, a.t + 1)
                dve.tensor_tensor(ctxm[:, :], ps_a[:, 0:P], head_mask[:, :], ALU.mult).then_inc(ctxm_done, 1)

            def residual(a, q=WHOLE):
                dve.wait_ge(q.of(attn_done), a.t + 1)
                dve.wait_ge(x_twice_done, a.t + 1)
                dve.tensor_tensor(res[:, q.c, :].rearrange("p c d -> p (c d)"), q.bank(spare_0)[:, q.n],
                                  x_twice[:, q.c, :].rearrange("p c d -> p (c d)"), ALU.add)\
                   .then_inc(q.of(res_done), 1)

            def first_stats(a, q=WHOLE):
                chunk_stats(res, stats, q.of(res_done), a.t + 1, stats_done, q)

            def first_means(a, q=WHOLE):
                chunk_means(stats, mv, a.t + 1, stats_done, mv_done, q)

            def first_norm(a, q=WHOLE):
                dve.wait_ge(q.of(rstd_done), a.t + 1)
                for c in q.chunks:
                    dve.tensor_scalar(x1[a.p][:, c, :], res[:, c, :], mv[:, c, 0:1], rstd[:, c:c + 1],
                                      ALU.subtract, ALU.mult).then_inc(x1_done, 1)

            def x1_low(a, q=WHOLE):
                dve.wait_ge(q.of(x1_hi_done), a.t + 1)
                dve.tensor_tensor(x1_lo[a.p][:, q.n], q.bank(spare_0)[:, q.n], x1_hi[a.p][:, q.n].bitcast(F32),
                                  ALU.subtract).then_inc(q.of(x1_lo_done), 1)

            def best_two(a):
                dve.wait_ge(logits_done, a.t + 1)
                parts = ps_a[:, 0:C * 2 * E].rearrange("p (c two e) -> p c two e", c=C, two=2)
                dve.tensor_copy(logits_lo[:, :, :], parts[:, :, 1, :]).then_inc(logits_lo_copied, 1)
                dve.wait_ge(logits_lo_copied, a.t + 1)
                dve.tensor_tensor(logits[:, :, :], parts[:, :, 0, :], logits_lo[:, :, :], ALU.add)\
                   .then_inc(logits_copied, 1)
                wait_apart(dve, logits_copied, a.t + 1)
                for c in range(C):
                    last = dve.max(top[:, c, :], logits[:, c, :])
                last.then_inc(top_done, 1)
                dve.wait_ge(top_done, a.t + 1)
                dve.tensor_tensor(gap[:, :], top[:, :, 1], top[:, :, 0], ALU.subtract).then_inc(gap_done, 1)

            def mark_two(a):
                for c in range(C):
                    last = dve.max_index(topi[:, c, :], top[:, c, :], logits[:, c, :])
                last.then_inc(topi_done, 1)
                dve.wait_ge(topi_done, a.t + 1)
                dve.tensor_tensor(chosen[:, :, :, :], iota[:, None, None, :].to_broadcast([P, C, 2, E]),
                                  topi[:, :, 0:2, None].to_broadcast([P, C, 2, E]), ALU.is_equal)\
                   .then_inc(chosen_done, 1)

            def combine_weights(a):
                dve.wait_ge(gap_exp_done, a.t + 1)
                dve.tensor_scalar(den[:, :], gap_exp[:, :], 1.0, None, ALU.add).then_inc(den_done, 1)
                dve.wait_ge(den_done, a.t + 1)
                dve.reciprocal(weights[:, :, 0], den[:, :]).then_inc(w0_done, 1)
                dve.wait_ge(w0_done, a.t + 1)
                dve.tensor_tensor(weights[:, :, 1], gap_exp[:, :], weights[:, :, 0], ALU.mult)\
                   .then_inc(weights_done, 1)
                dve.wait_ge(weights_done, a.t + 1)
                dve.wait_ge(chosen_done, a.t + 1)
                dve.tensor_tensor(chosen_w[:, :, :, :], chosen[:, :, :, :],
                                  weights[:, :, :, None].to_broadcast([P, C, 2, E]), ALU.mult)\
                   .then_inc(chosen_w_done, 1)
                dve.wait_ge(chosen_w_done, a.t + 1)
                dve.tensor_tensor(comb[:, :, :], chosen_w[:, :, 0, :], chosen_w[:, :, 1, :], ALU.add)\
                   .then_inc(comb_done, 1)

            def copy_y(t):
                dve.wait_ge(down_done, t.t * NH + NH)
                dve.tensor_copy(yT[:, :], ps_y[:, :]).then_inc(y_copied, 1)

            def last_residual(t, q=WHOLE, bank=ps_y):
                dve.wait_ge(q.of(y_turned), 1 if q.follows else t.t + 1)
                dve.tensor_tensor(res2[:, q.c, :].rearrange("p c d -> p (c d)"), bank[:, q.n],
                                  x1[t.p][:, q.c, :].rearrange("p c d -> p (c d)"), ALU.add)\
                   .then_inc(q.of(res2_done), 1)

            def last_stats(t, q=WHOLE):
                chunk_stats(res2, stats2, q.of(res2_done), 1 if q.follows else t.t + 1, stats2_done, q)

            def last_means(t, q=WHOLE):
                chunk_means(stats2, mv2, t.t + 1, stats2_done, mv2_done, q)

            def last_norm(t, q=WHOLE):
                dve.wait_ge(q.of(rstd2_done), 1 if q.follows else t.t + 1)
                if not (isinstance(t.t, int) and t.t == 0):
                    dve.wait_ge(out_stored, t.t * 16)
                for c in q.chunks:
                    last = dve.tensor_scalar(out_sb[:, c, :], res2[:, c, :], mv2[:, c, 0:1], rstd2[:, c:c + 1],
                                             ALU.subtract, ALU.mult)
                last.then_inc(q.of(out_ready), 1)

            def split_weights(e):
                dve.wait_ge(w_hi_done, e + 1)
                dve.tensor_tensor(w_lo[:, e, :], w_raw[:, e, :], w_hi[:, e, :].bitcast(F32), ALU.subtract)\
                   .then_inc(w_lo_dve, 1)

            def stats_x(b, q=WHOLE):
                chunk_stats(x_all[:, b, :, :], stats_all[:, b, :, :], x_loaded[b], 16, stats_all_done, q)
                chunk_means(stats_all[:, b, :, :], mv_all[:, b, :, :], b + 1, stats_all_done, mv_all_done, q)

            zero, one = Tile(0, 0), Tile(1, 1)
            for q in PARTS:
                stats_x(0, q)
            dve.wait_ge(router_hi_done, 1)
            dve.tensor_tensor(router[:, E:], router_raw, router[:, 0:E].bitcast(F32), ALU.subtract)\
               .then_inc(router_lo_done, 1)
            for q in PARTS:
                normalise(zero, q)
            stats_x(1)
            key_max(zero)
            split_weights(0)
            probabilities(zero)
            split_weights(1)
            stats_x(2)
            copy_av(zero)
            mask_heads(zero)
            normalise(one)
            split_weights(6)
            for q in PARTS:
                residual(zero, q)
                first_stats(zero, q)
                first_means(zero, q)
            key_max(one, spare_1)
            for q in PARTS:
                first_norm(zero, q)
            probabilities(one)
            for q in PARTS:
                x1_low(zero, q)
            split_weights(7)
            best_two(zero)
            mark_two(zero)
            copy_av(one, spare_1)
            combine_weights(zero)

            def product(t, j, last):
                n = t.t * NH + j
                dve.wait_ge(silu_done, n + 1)
                dve.wait_ge(u_done, n + 1)
                if not (isinstance(n, int) and n < R):
                    dve.wait_ge(h_lo_done, n - R + 1)
                dst = gated if half_at(j, last)[0] == 0 else hid
                dve.tensor_tensor(dst[j % R][:, :], ps_u[j % R][:, :], act_g[j % R][:, :], ALU.mult)\
                   .then_inc(hid_done, 1)

            def low(t, j):
                n = t.t * NH + j
                dve.wait_ge(h_hi_done, n + 1)
                dve.tensor_tensor(h_lo[j % RH][:, :], gated[j % R][:, :], h_hi[j % RH][:, :].bitcast(F32),
                                  ALU.subtract).then_inc(h_lo_done, 1)

            def step(t, first, last):
                a = None if last else t.next()
                S = FirstSlots if first else Slots
                for j in range(NH):
                    if not first and j == S.Y + 1:
                        last_residual(t.prev())
                    if not last:
                        if j == S.XT:
                            normalise(a)
                        if j == S.K + 1:
                            key_max(a)
                        if j == S.AV + 1:
                            copy_av(a)
                        if j == S.CTX + 1:
                            mask_heads(a)
                        if j == S.ATT + 1:
                            residual(a)
                        if j == S.ATT + 2:
                            first_stats(a)
                        if j == S.X1T:
                            first_norm(a)
                        if j == S.X1T + 1:
                            x1_low(a)
                        if j == S.ROUTE + 1:
                            best_two(a)
                        if j == S.COMB:
                            combine_weights(a)
                    if j >= 2:
                        low(t, j - 2)
                    elif not first:
                        low(t.prev(), NH - 2 + j)
                    if not first and j == LAG - 1:
                        copy_y(t.prev())
                    if not last and j == S.K + 2:
                        probabilities(a)
                    product(t, j, last)
                    if not last:
                        if j == S.ATT + 2:
                            first_means(a)
                        if j == S.ROUTE + 1:
                            mark_two(a)
                    if first:
                        if j == 2:
                            split_weights(SPLITS_DVE[-1])
                        if j in S.STATS:
                            stats_x(3 + S.STATS.index(j))
                    else:
                        if j == S.Y + 2:
                            last_stats(t.prev())
                        if j == S.Y + 3:
                            last_means(t.prev())
                        if j == S.Y + 6:
                            last_norm(t.prev())

            steps(dve, step)
            low(Tile(LAST, 1), NH - 2)
            low(Tile(LAST, 1), NH - 1)

            end = Tile(LAST, 1)
            for q in PARTS:
                last_residual(end, q, q.bank(ps_g[0]))
                last_stats(end, q)
                last_means(end, q)
            for q in PARTS:
                last_norm(end, q)

        @block.tensor
        def _(pe):
            def turn(dst, src, ready=None, count=0, q=WHOLE):
                for c in q.chunks:
                    if ready:
                        pe.wait_ge(ready, count + c + 1)
                    last = pe.transpose(dst[:, c * P:(c + 1) * P], src(c), ident[:, :])
                return last

            def turn_x(a, bank=ps_a):
                if not (isinstance(a.t, int) and a.t < 2):
                    pe.wait_ge(combT_copied, a.t)
                turn(bank, lambda c: xhat[:, c, :], xhat_done, a.t * C).then_inc(xhatT_done, 1)

            def keys(a, bank=ps_a):
                pe.wait_ge(xn_done, a.t + 1)
                pe.matmul(bank[:, :], wk, xnT[:, :], start=True, stop=True).then_inc(k_done, 1)

            def turn_prob(a, bank=ps_a):
                pe.wait_ge(probT_done, a.t + 1)
                turn(bank, lambda c: probT[:, c * P:(c + 1) * P]).then_inc(probt_done, 1)

            def weigh_x(a, bank=ps_a):
                pe.wait_ge(prob_done, a.t + 1)
                for c in range(C):
                    last = pe.matmul(bank[:, 0:P], xhat[:, c, :], prob[:, c, :], start=c == 0, stop=c == C - 1)
                last.then_inc(av_done, 1)

            def context(a):
                pe.wait_ge(av_copied, a.t + 1)
                if isinstance(a.t, int) and a.t == 1:
                    pe.wait_ge(combT_copied, 1)
                pe.matmul(ps_a[:, 0:P], wv, av[:, :], start=True, stop=True).then_inc(ctx_done, 1)

            def context_out(a):
                pe.wait_ge(ctxm_done, a.t + 1)
                pe.matmul(ps_a[:, 0:D], ctxm[:, :], wout, start=True, stop=True).then_inc(ctxo_done, 1)

            def mix_queries(a):
                pe.wait_ge(ctxo_copied, a.t + 1)
                pe.matmul(ps_a[:, 0:D], wqT, ctxo[:, :], start=True, stop=True).then_inc(mix_done, 1)

            def attend(a, q=WHOLE):
                pe.wait_ge(mix_copied, a.t + 1)
                for c in q.chunks:
                    last = pe.matmul(q.bank(spare_0)[:, c * D:(c + 1) * D], xnT[:, c * P:(c + 1) * P], mix[:, :],
                                     start=True, stop=True)
                last.then_inc(q.of(attn_done), 1)

            def turn_x1(a, q=WHOLE):
                turn(q.bank(spare_0), lambda c: x1[a.p][:, c, :], x1_done, a.t * C, q).then_inc(q.of(x1T_done), 1)

            def route(a, parts=(WHOLE,)):
                for q in parts:
                    pe.wait_ge(q.of(x1_lo_done), a.t + 1)
                    for c in q.chunks:
                        n, at = slice(c * P, (c + 1) * P), c * 2 * E
                        pe.matmul(ps_a[:, at:at + 2 * E], x1_hi[a.p][:, n], router[:, :],
                                  start=True, stop=False, skip_group_check=True)
                        last = pe.matmul(ps_a[:, at:at + E], x1_lo[a.p][:, n], router[:, 0:E],
                                         start=False, stop=True, skip_group_check=True)
                last.then_inc(logits_done, 1)

            def turn_comb(a):
                pe.wait_ge(comb_done, a.t + 1)
                pe.transpose(ps_a[0:C * E, 0:P], comb[:, :, :].rearrange("p c e -> p (c e)"), ident[:, :])\
                    .then_inc(combT_done, 1)

            def turn_y(t):
                pe.wait_ge(y_copied, t.t + 1)
                turn(ps_y, lambda c: yT[:, c * P:(c + 1) * P]).then_inc(y_turned, 1)

            def three(dst, e, col, hi, lo, start, stop):
                w = slice(col, col + P)
                pe.matmul(dst, w_hi[:, e, w], hi, start=start, stop=False)
                pe.matmul(dst, w_hi[:, e, w], lo, start=False, stop=False)
                return pe.matmul(dst, w_lo[:, e, w], hi, start=False, stop=stop)

            def up(t, j, first, last):
                e, h = half_at(j, last)
                n = t.t * NH + j
                if j == 0:
                    pe.wait_ge(x1_lo_done, t.t + 1)
                if first and h == 0:
                    if e in SPLITS_DVE:
                        pe.wait_ge(w_lo_dve, SPLITS_DVE.index(e) + 1)
                    else:
                        pe.wait_ge(w_lo_pool, SPLITS_POOL.index(e) + 1)
                free = not (isinstance(n, int) and n < R)
                if free:
                    pe.wait_ge(silu_done, n - R + 1)
                three(ps_g[j % R][:, :], e, h * P, x1_hi[t.p][:, :], x1_lo[t.p][:, :], True, True)\
                    .then_inc(g_done, 1)
                if free:
                    pe.wait_ge(hid_done, n - R + 1)
                elif ps_u[j] is spare_1:
                    pe.wait_ge(av_copied, 2)
                three(ps_u[j % R][:, :], e, H + h * P, x1_hi[t.p][:, :], x1_lo[t.p][:, :], True, True)\
                    .then_inc(u_done, 1)

            def down(t, j, last=False):
                e, h = half_at(j, last)
                pe.wait_ge(h_lo_done, t.t * NH + j + 1)
                if j == 0 and not (isinstance(t.t, int) and t.t == 0):
                    pe.wait_ge(res2_done, t.t)
                three(ps_y[:, :], e, WD + h * P, h_hi[j % RH][:, :], h_lo[j % RH][:, :], j == 0, j == NH - 1)\
                    .then_inc(down_done, 1)

            def keep_clock(n):
                for _ in range(n):
                    pe.matmul(ps_y[:, 0:P], ident[:, :], ident[:, :], start=True, stop=True)

            zero, one = Tile(0, 0), Tile(1, 1)
            pe.wait_ge(consts_done, 1)
            keep_clock(11)
            turn_x(zero)
            pe.wait_ge(small_loaded, 16)
            keep_clock(3)
            keys(zero)
            keep_clock(9)
            turn_prob(zero)
            keep_clock(3)
            weigh_x(zero)
            keep_clock(3)
            context(zero)
            keep_clock(2)
            context_out(zero)
            keep_clock(3)
            mix_queries(zero)
            keep_clock(3)
            for q in PARTS:
                attend(zero, q)
            turn_x(one, spare_1)
            keep_clock(3)
            keys(one, spare_1)
            keep_clock(6)
            for q in PARTS:
                turn_x1(zero, q)
            turn_prob(one, spare_1)
            keep_clock(3)
            pe.wait_ge(router_lo_done, 1)
            route(zero, PARTS)
            weigh_x(one, spare_1)

            def step(t, first, last):
                a = None if last else t.next()
                S = FirstSlots if first else Slots
                for j in range(NH):
                    up(t, j, first, last)
                    if j >= S.DOWN:
                        for i in range(0 if j == S.DOWN else j - LAG, j - LAG + 1):
                            down(t, i, last)
                    elif j < LAG and not first:
                        down(t.prev(), NH - LAG + j)
                    if first and j == S.COMB0:
                        turn_comb(t)
                    if not first and j == S.Y:
                        turn_y(t.prev())
                    if not last:
                        if j == S.XT:
                            turn_x(a)
                        if j == S.K:
                            keys(a)
                        if j == S.PROB:
                            turn_prob(a)
                        if j == S.AV:
                            weigh_x(a)
                        if j == S.CTX:
                            context(a)
                        if j == S.CTXO:
                            context_out(a)
                        if j == S.MIX:
                            mix_queries(a)
                        if j == S.ATT:
                            attend(a)
                        if j == S.X1T:
                            turn_x1(a)
                        if j == S.ROUTE:
                            route(a)
                        if j == S.COMB:
                            turn_comb(a)

            steps(pe, step)
            end = Tile(LAST, 1)
            for j in range(NH - LAG, NH):
                down(end, j, True)
            for q in PARTS:
                pe.wait_ge(q.of(y_copied), 1 if q.follows else B)
                turn(q.bank(ps_g[0]), lambda c: yT[:, c * P:(c + 1) * P], q=q).then_inc(q.of(y_turned), 1)


def kernel(**inputs):
    import numpy as np
    import concourse.bacc as bacc
    from concourse import mybir as mb
    from concourse.bass_utils import run_bass_kernel_spmd

    a = {k: np.asarray(v) for k, v in inputs.items()}
    D = a["L0_attn_x"].shape[2]
    hidden = a["L0_attn_w_qkv"].shape[1] // 3
    w = a["L0_attn_w_qkv"]

    def up(m):
        return np.swapaxes(m, -1, -2)

    def down(m):
        m = np.swapaxes(m, -1, -2)
        m = m.reshape(*m.shape[:-2], m.shape[-2] // 128, 128, D)
        m = np.swapaxes(m, -3, -2)
        return m.reshape(*m.shape[:-2], -1)

    shared = np.concatenate([up(a["L0_ffn_sg"]), up(a["L0_ffn_su"]), down(a["L0_ffn_sd"])], axis=-1)
    routed = np.concatenate([up(a["L0_ffn_Wg"]), up(a["L0_ffn_Wu"]), down(a["L0_ffn_Wd"])], axis=-1)
    small = [w[:, hidden:2 * hidden], w[:, 2 * hidden:], a["L0_attn_w_out"], w[:, 0:hidden].T,
             a["L0_ffn_w_router"].T, a["L0_attn_gamma"].reshape(D, 1), a["L0_attn_beta"].reshape(D, 1)]
    arrays = {
        "x": a["L0_attn_x"],
        "small": np.concatenate(small, axis=1),
        "bout": a["L0_attn_b_out"],
        "experts": np.concatenate([shared[None], routed], axis=0),
    }
    arrays = {k + "_in": np.ascontiguousarray(v) for k, v in arrays.items()}
    nc = bacc.Bacc("TRN2", target_bir_lowering=False, num_devices=1)
    args = [nc.dram_tensor(k, v.shape, mb.dt.from_np(v.dtype), kind="ExternalInput").ap()
            for k, v in arrays.items()]
    out = nc.dram_tensor("out", a["L0_attn_x"].shape, mb.dt.float32, kind="ExternalOutput").ap()
    build(nc, *args, out)
    r = run_bass_kernel_spmd(nc, [arrays], core_ids=[0])
    return r.results[0]["out"]
```
